# Optimizing a Trainium2 kernel written in Bass

```python
import numpy as np
import jax
import jax.numpy as jnp

def _softmax(x, axis=-1):
    return jax.nn.softmax(x, axis=axis)

def _gelu(x):
    return jax.nn.gelu(x, approximate=True)

def _silu(x):
    return jax.nn.silu(x)

def _sigmoid(x):
    return jax.nn.sigmoid(x)

def _layernorm(x, axis=-1, eps=1e-05):
    m = jnp.mean(x, axis=axis, keepdims=True)
    v = jnp.var(x, axis=axis, keepdims=True)
    return (x - m) / jnp.sqrt(v + eps)

def _scatter_add(tgt, idx, src, axis=0):
    return tgt.at[idx].add(src)

def _segment_sum(src, seg, n):
    return jax.ops.segment_sum(src, seg, n)
kernel_name = 'mk_gnn_resnorm_d2_gnn_r8_a71037'

def setup_inputs(seed: int=0):
    np.random.seed(seed)
    _w = jnp.asarray

    def _rec_inputs():
        import jax
        import jax.numpy as jnp
        _gk = jax.random.key(seed)
        x = -0.000202 + 1 * jax.random.normal(jax.random.fold_in(_gk, 1), (12500, 64), jnp.float32)
        src = jax.random.randint(jax.random.fold_in(_gk, 2), (400000,), 0, 12500, jnp.int32)
        dst = jnp.minimum((12500 * jax.random.uniform(jax.random.fold_in(_gk, 3), (400000,)) ** 2.0).astype(jnp.int32), 99999)
        _o = jnp.argsort(dst, stable=True)
        src = src[_o]
        dst = dst[_o]
        edge_attr_64 = -0.000129727 + 1.00004 * jax.random.normal(jax.random.fold_in(_gk, 12), (400000, 64), jnp.float32)
        return (x, src, dst, edge_attr_64)
    x, src, dst, edge_attr_64 = _rec_inputs()

    def _L0_gnn_setup():
        import jax, jax.numpy as jnp
        import numpy as np
        N_NODES = 12500

        def mean_aggregate(x, src, dst, num_nodes):
            msgs = x[src]
            summed = jax.ops.segment_sum(msgs, dst, num_segments=num_nodes)
            deg = jax.ops.segment_sum(jnp.ones((src.shape[0],), x.dtype), dst, num_segments=num_nodes)
            deg = jnp.maximum(deg, 1.0)
            return summed / deg[:, None]
        key = jax.random.key(seed)
        ks = jax.random.split(key, 8)
        F, H, C = (64, 16, 64)
        E = 125000
        x = jax.random.normal(ks[0], (N_NODES, F), dtype=jnp.float32)
        edge_index = jax.random.randint(ks[1], (2, E), 0, N_NODES, dtype=jnp.int64)
        s = 1.0 / np.sqrt(F)
        sh = 1.0 / np.sqrt(H)
        return {'x': x, 'edge_index': edge_index, 'W_lin': jax.random.normal(ks[2], (F, C), jnp.float32) * s, 'b_lin': jnp.zeros((C,), jnp.float32), 'W1_agg': jax.random.normal(ks[3], (C, H), jnp.float32) * s, 'W1_root': jax.random.normal(ks[4], (C, H), jnp.float32) * s, 'b1': jnp.zeros((H,), jnp.float32), 'W2_agg': jax.random.normal(ks[5], (H, C), jnp.float32) * sh, 'W2_root': jax.random.normal(ks[6], (H, C), jnp.float32) * sh, 'b2': jnp.zeros((C,), jnp.float32)}
    _L0_gnn_all = _L0_gnn_setup()
    _L0_gnn_in = {k: v for k, v in _L0_gnn_all.items() if k in ('W_lin', 'b_lin', 'W1_agg', 'W1_root', 'b1', 'W2_agg', 'W2_root', 'b2')}
    del _L0_gnn_all

    def _L1_gnn_setup():
        import jax, jax.numpy as jnp
        import numpy as np
        LOG2 = float(np.log(2.0))

        def ssp(x):
            return jax.nn.softplus(x) - LOG2
        V, E, F, EIN, H = (6250, 100000, 64, 64, 64)
        key = jax.random.key(seed)
        ks = jax.random.split(key, 16)

        def lin(k, out_d, in_d):
            bound = 1.0 / np.sqrt(in_d)
            k1, k2 = jax.random.split(k)
            W = jax.random.uniform(k1, (out_d, in_d), jnp.float32, -bound, bound)
            b = jax.random.uniform(k2, (out_d,), jnp.float32, -bound, bound)
            return (W, b)
        Wn, bn = lin(ks[0], H, F)
        We1, be1 = lin(ks[1], H, EIN)
        We2, be2 = lin(ks[2], H, H)
        Wc, bc = lin(ks[3], F, H)
        Wp, bp = lin(ks[4], F, F)
        return {'node_feats_in': jax.random.normal(ks[5], (V, F), jnp.float32), 'edge_feats': jax.random.normal(ks[6], (E, EIN), jnp.float32), 'src': jax.random.randint(ks[7], (E,), 0, V, jnp.int32), 'dst': jax.random.randint(ks[8], (E,), 0, V, jnp.int32), 'Wn': Wn, 'bn': bn, 'We1': We1, 'be1': be1, 'We2': We2, 'be2': be2, 'Wc': Wc, 'bc': bc, 'Wp': Wp, 'bp': bp}
    _L1_gnn_all = _L1_gnn_setup()
    _L1_gnn_in = {k: v for k, v in _L1_gnn_all.items() if k in ('Wn', 'bn', 'We1', 'be1', 'We2', 'be2', 'Wc', 'bc', 'Wp', 'bp')}
    del _L1_gnn_all
    return {'x': x, 'src': src, 'dst': dst, 'edge_attr_64': edge_attr_64, 'L0_gnn_W_lin': _L0_gnn_in['W_lin'], 'L0_gnn_b_lin': _L0_gnn_in['b_lin'], 'L0_gnn_W1_agg': _L0_gnn_in['W1_agg'], 'L0_gnn_W1_root': _L0_gnn_in['W1_root'], 'L0_gnn_b1': _L0_gnn_in['b1'], 'L0_gnn_W2_agg': _L0_gnn_in['W2_agg'], 'L0_gnn_W2_root': _L0_gnn_in['W2_root'], 'L0_gnn_b2': _L0_gnn_in['b2'], 'L1_gnn_Wn': _L1_gnn_in['Wn'], 'L1_gnn_bn': _L1_gnn_in['bn'], 'L1_gnn_We1': _L1_gnn_in['We1'], 'L1_gnn_be1': _L1_gnn_in['be1'], 'L1_gnn_We2': _L1_gnn_in['We2'], 'L1_gnn_be2': _L1_gnn_in['be2'], 'L1_gnn_Wc': _L1_gnn_in['Wc'], 'L1_gnn_bc': _L1_gnn_in['bc'], 'L1_gnn_Wp': _L1_gnn_in['Wp'], 'L1_gnn_bp': _L1_gnn_in['bp']}

def reference(x, src, dst, edge_attr_64, L0_gnn_W_lin, L0_gnn_b_lin, L0_gnn_W1_agg, L0_gnn_W1_root, L0_gnn_b1, L0_gnn_W2_agg, L0_gnn_W2_root, L0_gnn_b2, L1_gnn_Wn, L1_gnn_bn, L1_gnn_We1, L1_gnn_be1, L1_gnn_We2, L1_gnn_be2, L1_gnn_Wc, L1_gnn_bc, L1_gnn_Wp, L1_gnn_bp):
    import jax
    import jax.numpy as jnp

    def _L0_gnn_ref(x, edge_index, W_lin, b_lin, W1_agg, W1_root, b1, W2_agg, W2_root, b2):
        import jax, jax.numpy as jnp
        import numpy as np
        N_NODES = 12500

        def mean_aggregate(x, src, dst, num_nodes):
            msgs = x[src]
            summed = jax.ops.segment_sum(msgs, dst, num_segments=num_nodes)
            deg = jax.ops.segment_sum(jnp.ones((src.shape[0],), x.dtype), dst, num_segments=num_nodes)
            deg = jnp.maximum(deg, 1.0)
            return summed / deg[:, None]
        src, dst = (edge_index[0], edge_index[1])
        h = x @ W_lin + b_lin
        agg1 = mean_aggregate(h, src, dst, N_NODES)
        h = jnp.tanh(agg1 @ W1_agg + h @ W1_root + b1)
        agg2 = mean_aggregate(h, src, dst, N_NODES)
        out = jnp.tanh(agg2 @ W2_agg + h @ W2_root + b2)
        return out

    def _L1_gnn_ref(node_feats_in, edge_feats, src, dst, Wn, bn, We1, be1, We2, be2, Wc, bc, Wp, bp):
        import jax, jax.numpy as jnp
        import numpy as np
        LOG2 = float(np.log(2.0))

        def ssp(x):
            return jax.nn.softplus(x) - LOG2
        V = node_feats_in.shape[0]
        h = node_feats_in @ Wn.T + bn
        h_src = h[src]
        w = ssp(edge_feats @ We1.T + be1)
        w = ssp(w @ We2.T + be2)
        m = h_src * w
        agg = jax.ops.segment_sum(m, dst, num_segments=V)
        out = ssp(agg @ Wc.T + bc)
        return out @ Wp.T + bp
    edge_index = jnp.stack([src, dst])
    x = _layernorm(x + _L0_gnn_ref(x, edge_index, L0_gnn_W_lin, L0_gnn_b_lin, L0_gnn_W1_agg, L0_gnn_W1_root, L0_gnn_b1, L0_gnn_W2_agg, L0_gnn_W2_root, L0_gnn_b2), axis=-1)
    x = _layernorm(x + _L1_gnn_ref(x, edge_attr_64, src, dst, L1_gnn_Wn, L1_gnn_bn, L1_gnn_We1, L1_gnn_be1, L1_gnn_We2, L1_gnn_be2, L1_gnn_Wc, L1_gnn_bc, L1_gnn_Wp, L1_gnn_bp), axis=-1)
    return x

_drawn_inputs = setup_inputs


def setup_inputs(seed=0):
    import zlib

    import numpy as np

    out = dict(_drawn_inputs(seed))
    spreads = {'L0_gnn_b_lin': (0.0, 0.1), 'L0_gnn_b1': (0.0, 0.1), 'L0_gnn_b2': (0.0, 0.1)}
    factors = {'L1_gnn_be1': 5.555, 'L1_gnn_bc': 2.736}
    for name, (base, spread) in spreads.items():
        noise = np.random.default_rng([zlib.crc32(name.encode()), seed]).standard_normal(out[name].shape)
        drawn = base * np.exp(spread * noise) if base else spread * noise
        out[name] = jnp.asarray(drawn.astype(out[name].dtype))
    for name, factor in factors.items():
        out[name] = (out[name] * factor).astype(out[name].dtype)
    return out
```

```python
import concourse.bass as bass
import concourse.mybir as mybir
from contextlib import ExitStack

F32 = mybir.dt.float32
I32 = mybir.dt.int32
ALU = mybir.AluOpType
ACT = mybir.ActivationFunctionType
AX = mybir.AxisListType

P = 128
V = 12500
E = 400000
F = 64
H = 16
LOG2 = 0.6931471805599453
EPS = 1e-5

SLOTS = 25
EB = P * SLOTS
NB = E // EB
PAIRS = (SLOTS + 1) // 2
HALVES = ((0, 13), (13, SLOTS))
GROUPS = ((0, 4), (4, 7), (7, 10), (10, 13))
NG = len(GROUPS)

WIN = 128
NW = -(-V // WIN)
VP = NW * WIN

SUB = 125
NSUB = 4
CH = SUB * NSUB
NC = V // CH
assert NB * EB == E and NC * CH == V

MSG0 = 48
ONES_AT = 32


def gnn_kernel(nc, x, src, dst, edge, W_lin, b_lin, W1_agg, W1_root, b1, W2_agg, W2_root, b2,
               WnT, bn, We1T, be1, We2T, be2, WcT, bc, WpT, bp, out):
    ctx = ExitStack()
    with ctx:
        def sb(name, shape, dt=F32):
            return ctx.enter_context(nc.sbuf_tensor(name, shape, dt))

        def pb(name, shape):
            return ctx.enter_context(nc.psum_tensor(name, shape, F32))

        def sem(name):
            return ctx.enter_context(nc.semaphore(name))

        p1_table = nc.dram_tensor("p1_table", (V, H), F32).ap()
        h1_table = nc.dram_tensor("h1_table", (V, H), F32).ap()
        hn_table = nc.dram_tensor("hn_table", (V, F), F32).ap()

        src_v = src.rearrange("(n p j) -> n p j", p=P, j=SLOTS)
        dst_v = dst.rearrange("(n p j) -> p n j", p=P, j=SLOTS)
        edge_v = edge.rearrange("(n p j) f -> n p (j f)", p=P, j=SLOTS)

        def chunks(t):
            return t.rearrange("(c s q) f -> c q s f", s=NSUB, q=SUB)

        x_v, out_v = chunks(x), chunks(out)
        p1_v, h1_v, hn_v = chunks(p1_table), chunks(h1_table), chunks(hn_table)

        ident = sb("ident", [P, P])
        iota_i = sb("iota_i", [P, P], I32)
        iota_row = sb("iota_row", [P, WIN])
        win_base_i = sb("win_base_i", [P, NW], I32)
        win_base = sb("win_base", [P, NW])
        upto = sb("upto", [P, P])
        zeros = sb("zeros", [F, CH])
        ones_row = sb("ones_row", [1, P])
        ones_blk = sb("ones_blk", [F, P])

        w_lin = sb("w_lin", [F, F])
        w1a = sb("w1a", [F, H])
        w1r = sb("w1r", [F, H])
        w2a = sb("w2a", [H, F])
        w2r = sb("w2r", [H, F])
        wn = sb("wn", [F, F])
        wc = sb("wc", [F, 2 * F])
        wp = sb("wp", [F, F])
        we2 = sb("we2", [F, F])
        we1_2 = sb("we1_2", [P, P])
        we2_2 = sb("we2_2", [P, P])
        c_lin = sb("c_lin", [F, 1])
        c_b1 = sb("c_b1", [H, 1])
        c_be1 = sb("c_be1", [P, 1])
        n_be1 = sb("n_be1", [P, 1])
        c_bc = sb("c_bc", [F, 1])
        n_bc = sb("n_bc", [F, 1])
        bc_off = sb("bc_off", [F, 1])
        be1_off = sb("be1_off", [F, 1])
        be1_wide = sb("be1_wide", [F, P])
        r_b2 = sb("r_b2", [1, F])
        r_bn = sb("r_bn", [1, F])
        r_be2 = sb("r_be2", [1, F])
        r_bp = sb("r_bp", [1, F])
        be2_wide = sb("be2_wide", [P, 8 * F])

        dst_f = sb("dst_f", [P, NB, SLOTS])
        dst_ext = sb("dst_ext", [P, 2, NB])
        ext_t = sb("ext_t", [NB, 2])
        ext_i = sb("ext_i", [NB, 2], I32)
        win_lo = sb("win_lo", [NB, 1])
        win_hi = sb("win_hi", [NB, 1])
        win_n = sb("win_n", [NB, 1])
        win_row = sb("win_row", [1, NB])
        visits = sb("visits", [1, 3 * NB], I32)

        src_i = [sb(f"src_i{u}", [P, SLOTS], I32) for u in range(2)]
        hot = [sb(f"hot{h}", [P, b - a, WIN]) for h, (a, b) in enumerate(HALVES)]
        big = sb("big", [P, 2, SLOTS * F])
        rows = [big[:, u, :].rearrange("p (j f) -> p j f", f=F) for u in range(2)]
        msgs = [big[:, u, 0:SLOTS * MSG0].rearrange("p (j f) -> p j f", f=MSG0) for u in range(2)]

        acc = sb("acc", [F, VP])
        shared = sb("shared", [P, V])
        hT = shared[0:H, :]
        XE = (SLOTS + 1) * F
        x_e = [shared[:, u * XE:(u + 1) * XE] for u in range(2)]
        xT_e, lg1, s1, gate_e, lg2 = (shared[:, k * XE:(k + 1) * XE] for k in range(2, 7))
        x1 = sb("x1", [SUB, NC * NSUB, F])

        x_n = [sb(f"x_n{b}", [SUB, NSUB, F]) for b in range(2)]
        nT = sb("nT", [F, CH])
        nT2 = sb("nT2", [F, CH])
        h_chunk = sb("h_chunk", [H, CH])
        inv_deg = sb("inv_deg", [H, CH])
        o_small = [sb(f"o_small{b}", [SUB, NSUB, H]) for b in range(2)]
        o_wide = [sb(f"o_wide{b}", [SUB, NSUB, F]) for b in range(2)]
        yv = sb("yv", [SUB, NSUB, F])
        sq = sb("sq", [SUB, NSUB, F])
        st_sum = sb("st_sum", [SUB, NSUB])
        st_mean = sb("st_mean", [SUB, NSUB])
        st_var = sb("st_var", [SUB, NSUB])
        st_rstd = sb("st_rstd", [SUB, NSUB])
        x1_var = sb("x1_var", [SUB, NC * NSUB])
        x1_rstd = sb("x1_rstd", [SUB, NC * NSUB])

        bank = [pb(f"bank{i}", [P, 512]) for i in range(8)]

        waited = sem("waited")

        weights_in = sem("weights_in")
        dst_in = sem("dst_in")
        iotas = sem("iotas")
        consts = sem("consts")
        small = sem("small")
        ext_psum = sem("ext_psum")
        ext_sb = sem("ext_sb")
        visit_psum = sem("visit_psum")
        be2_psum = sem("be2_psum")
        setup_done = sem("setup_done")
        a_x_in = [sem(f"a_x_in{b}") for b in range(2)]
        a_x_used = sem("a_x_used")
        a_xT_psum = sem("a_xT_psum")
        a_xT = sem("a_xT")
        a_h_psum = sem("a_h_psum")
        a_h = sem("a_h")
        a_p_psum = sem("a_p_psum")
        a_out = sem("a_out")
        a_root = sem("a_root")
        a_store = [sem(f"a_store{b}") for b in range(2)]

        loads = [(w_lin[:, :], W_lin), (w1a[:, :], W1_agg), (w1r[:, :], W1_root), (w2a[:, :], W2_agg),
                 (w2r[:, :], W2_root), (wn[:, :], WnT), (wc[:, 0:F], WcT), (wc[:, F:2 * F], WcT), (wp[:, :], WpT), (we2[:, :], We2T),
                 (c_lin[:, :], b_lin), (c_b1[:, :], b1), (c_bc[:, :], bc),
                 (c_be1[0:F, :], be1), (c_be1[F:P, :], be1),
                 (r_b2[:, :], b2), (r_bn[:, :], bn), (r_be2[:, :], be2), (r_bp[:, :], bp)]
        corners = [(we1_2[0:F, 0:F], We1T), (we1_2[F:P, F:P], We1T),
                   (we2_2[0:F, 0:F], We2T), (we2_2[F:P, F:P], We2T)]
        ALL_IN = 16 * (len(loads) + len(corners))

        with nc.Block() as block:
            @block.sync
            def _(sp):
                def load_x(c, b):
                    sp.wait_ge(a_x_used, c + 1)
                    sp.dma_start(x_n[b][:, :, :], x_v[c]).then_inc(a_x_in[b], 16)

                def store_p1(c, b):
                    sp.wait_ge(a_out, c + 2)
                    sp.dma_start(p1_v[c], o_small[b][:, :, :]).then_inc(a_store[b], 16)

                load_x(0, 0)
                sp.dma_start(dst_f[:, :, :].bitcast(I32), dst_v).then_inc(dst_in, 16)
                with sp.Fori(0, NC // 2) as g:
                    load_x(2 * g + 1, 1)
                    store_p1(2 * g, 0)
                    load_x(2 * g + 2, 0)
                    store_p1(2 * g + 1, 1)
                store_p1(NC - 1, 0)
                sp.wait_ge(a_store[0], 16 * (NC // 2 + 1))
                sp.wait_ge(a_store[1], 16 * (NC // 2))

            @block.gpsimd
            def _(pool):
                pool.memset(ident[:, :], 0.0)
                pool.memset(upto[:, :], 1.0)
                pool.memset(zeros[:, :], 0.0)
                pool.memset(ones_row[:, :], 1.0)
                pool.memset(ones_blk[:, :], 1.0)
                pool.memset(we1_2[:, :], 0.0)
                pool.memset(we2_2[:, :], 0.0)
                pool.iota(iota_i[:, :], pattern=[[1, WIN]], base=0, channel_multiplier=0)
                pool.iota(win_base_i[:, :], pattern=[[WIN, NW]], base=0, channel_multiplier=0).then_inc(iotas, 1)
                pool.wait_ge(iotas, 1)
                pool.affine_select(out=ident[:, :], in_=ident[:, :], compare_op=ALU.not_equal, fill=1.0,
                                   base=0, pattern=[[-1, P]], channel_multiplier=1)
                pool.affine_select(out=upto[:, :], in_=upto[:, :], compare_op=ALU.is_ge, fill=0.0,
                                   base=0, pattern=[[1, P]], channel_multiplier=-1)
                pool.memset(acc[:, :], 0.0)
                pool.memset(big[:, :, :], 1.0).then_inc(consts, 1)

            @block.scalar
            def _(act):
                for tile, dram in loads:
                    act.dma_start(tile, dram).then_inc(weights_in, 16)
                act.wait_ge(iotas, 1)
                for tile, dram in corners:
                    act.dma_start(tile, dram).then_inc(weights_in, 16)
                act.wait_ge(weights_in, ALL_IN)

                def chunk(c):
                    act.wait_ge(a_xT_psum, c + 1)
                    act.copy(nT[:, :], bank[0][0:F, 0:CH]).then_inc(a_xT, 1)
                    act.wait_ge(a_h_psum, c + 1)
                    act.activation(nT2[:, :], bank[1][0:F, 0:CH], ACT.Identity,
                                   bias=c_lin[:, :]).then_inc(a_h, 1)

                with act.Fori(0, NC) as c:
                    chunk(c)

            @block.tensor
            def _(pe):
                pe.wait_ge(consts, 1)
                pe.wait_ge(weights_in, ALL_IN)
                pe.sem_inc(a_x_used, 2)

                def chunk(c, g, b):
                    pe.wait_ge(a_x_in[b], 16 * (g + 1))
                    pe.sem_inc(waited, 1)
                    for s in range(NSUB):
                        last = pe.transpose(bank[0][0:F, s * SUB:(s + 1) * SUB], x_n[b][:, s, :],
                                            ident[0:SUB, 0:SUB])
                    last.then_inc(a_xT_psum, 1)
                    pe.wait_ge(a_xT_psum, c + 1)
                    pe.sem_inc(a_x_used, 1)
                    pe.wait_ge(a_xT, c + 1)
                    pe.sem_inc(waited, 1)
                    pe.matmul(bank[1][0:F, 0:CH], w_lin[:, :], nT[:, :], start=True,
                              stop=True).then_inc(a_h_psum, 1)
                    pe.wait_ge(a_h, c + 1)
                    pe.wait_ge(a_out, c + 1)
                    pe.sem_inc(waited, 1)
                    for s in range(NSUB):
                        pe.matmul(bank[2][0:SUB, s * H:(s + 1) * H], nT2[:, s * SUB:(s + 1) * SUB], w1a[:, :],
                                  start=True, stop=True)
                    pe.matmul(bank[3][0:H, 0:CH], w1r[:, :], nT2[:, :], start=True,
                              stop=True).then_inc(a_p_psum, 1)

                with pe.Fori(0, NC // 2) as g:
                    for b in range(2):
                        chunk(2 * g + b, g, b)
                chunk(NC - 1, NC // 2, 0)
                pe.wait_ge(small, 1)
                for k in range(2):
                    last = pe.transpose(bank[4][0:NB, k * P:(k + 1) * P], dst_ext[:, k, :], ident[:, :])
                last.then_inc(ext_psum, 1)
                pe.wait_ge(ext_sb, 1)
                pe.matmul(bank[5][0:1, 0:NB], win_n[:, :], upto[0:NB, 0:NB], start=True, stop=True)
                pe.matmul(bank[5][0:1, NB:2 * NB], win_n[:, :], ident[0:NB, 0:NB], start=True, stop=True)
                pe.matmul(bank[5][0:1, 2 * NB:3 * NB], win_lo[:, :], ident[0:NB, 0:NB], start=True,
                          stop=True).then_inc(visit_psum, 1)
                pe.matmul(bank[6][:, 0:F], be1_wide[:, :], we2[:, :], start=True, stop=False)
                pe.matmul(bank[6][:, 0:F], ones_row[:, :], r_be2[:, :], start=False,
                          stop=True).then_inc(be2_psum, 1)

            @block.vector
            def _(dve):
                dve.wait_ge(iotas, 1)
                dve.tensor_copy(iota_row[:, :], iota_i[:, :])
                dve.tensor_copy(win_base[:, :], win_base_i[:, :])
                dve.wait_ge(weights_in, ALL_IN)
                dve.wait_ge(consts, 1)
                dve.tensor_scalar(n_be1[:, :], c_be1[:, :], -1.0, None, ALU.mult)
                dve.tensor_scalar(n_bc[:, :], c_bc[:, :], -1.0, None, ALU.mult)
                dve.tensor_scalar(bc_off[:, :], c_bc[:, :], -LOG2, None, ALU.add)
                dve.tensor_scalar(be1_off[:, :], c_be1[0:F, :], -LOG2, None, ALU.add)
                dve.drain()
                dve.tensor_scalar(be1_wide[:, :], ones_blk[:, :], be1_off[:, :], None, ALU.mult)

                dve.sem_inc(a_out, 1)

                def chunk(c, g, b):
                    dve.wait_ge(a_p_psum, c + 1)
                    if not isinstance(g, int) or g > 0:
                        dve.wait_ge(a_store[b], 16 * g)
                    dve.tensor_scalar(hT[:, bass.ds(c * CH, CH)], bank[3][0:H, 0:CH], c_b1[:, :], None, ALU.add)
                    dve.tensor_copy(o_small[b][:, :, :],
                                    bank[2][0:SUB, 0:NSUB * H].rearrange("q (s f) -> q s f", f=H)).then_inc(a_out, 1)

                chunk(0, 0, 0)
                chunk(1, 0, 1)
                with dve.Fori(1, NC // 2) as g:
                    for b in range(2):
                        chunk(2 * g + b, g, b)
                chunk(NC - 1, NC // 2, 0)

                dve.wait_ge(dst_in, 16)
                dve.tensor_copy(dst_f[:, :, :], dst_f[:, :, :].bitcast(I32))
                dve.drain()
                dve.tensor_reduce(dst_ext[:, 0, :], dst_f[:, :, :], AX.X, ALU.min)
                dve.tensor_reduce(dst_ext[:, 1, :], dst_f[:, :, :], AX.X, ALU.max).then_inc(small, 1)
                dve.wait_ge(ext_psum, 1)
                dve.tensor_reduce(ext_t[:, 0:1], bank[4][0:NB, 0:P], AX.X, ALU.min)
                dve.tensor_reduce(ext_t[:, 1:2], bank[4][0:NB, P:2 * P], AX.X, ALU.max)
                dve.drain()
                dve.tensor_copy(ext_i[:, :], ext_t[:, :])
                dve.drain()
                dve.tensor_single_scalar(ext_i[:, :], ext_i[:, :], WIN.bit_length() - 1, ALU.arith_shift_right)
                dve.drain()
                dve.tensor_copy(win_lo[:, :], ext_i[:, 0:1])
                dve.tensor_copy(win_hi[:, :], ext_i[:, 1:2])
                dve.drain()
                dve.scalar_tensor_tensor(win_n[:, :], win_hi[:, :], 1.0, win_lo[:, :], ALU.add,
                                         ALU.subtract).then_inc(ext_sb, 1)
                dve.wait_ge(visit_psum, 1)
                dve.tensor_copy(win_row[:, :], bank[5][0:1, NB:2 * NB])
                dve.tensor_copy(visits[:, NB:2 * NB], bank[5][0:1, 0:NB])
                dve.tensor_copy(visits[:, 2 * NB:3 * NB], bank[5][0:1, 2 * NB:3 * NB])
                dve.drain()
                dve.tensor_tensor(visits[:, 0:NB], bank[5][0:1, 0:NB], win_row[:, :], ALU.subtract)
                dve.wait_ge(be2_psum, 1)
                for k in range(8):
                    dve.tensor_copy(be2_wide[:, k * F:(k + 1) * F], bank[6][:, 0:F])

        def windows(eng, n, with_first):
            since = eng.value_load(visits[0:1, bass.ds(n, 1)], min_val=0, max_val=NB * NW - 1)
            to = eng.value_load(visits[0:1, bass.ds(n + NB, 1)], min_val=1, max_val=NB * NW)
            if not with_first:
                return since, to, None
            first = eng.value_load(visits[0:1, bass.ds(n + 2 * NB, 1)], min_val=0, max_val=NW - 1)
            return since, to, first

        def edge_phase(tag, table, buf, width, cols, with_edges):
            idx_in = [sem(f"{tag}_idx_in{u}") for u in range(2)]
            gathered = [sem(f"{tag}_gathered{u}") for u in range(2)]
            block_used = sem(f"{tag}_block_used")
            hot_made = [sem(f"{tag}_hot_made{h}") for h in range(2)]
            hot_used = [sem(f"{tag}_hot_used{h}") for h in range(2)]
            acc_added = sem(f"{tag}_acc_added")
            sums = bank[7]
            if with_edges:
                e_in = [sem(f"{tag}_e_in{u}") for u in range(2)]
                e_used = sem(f"{tag}_e_used")
                xT_psum = sem(f"{tag}_xT_psum")
                xT_made = sem(f"{tag}_xT_made")
                z1_psum = sem(f"{tag}_z1_psum")
                log1_made = sem(f"{tag}_log1_made")
                s1_made = sem(f"{tag}_s1_made")
                z2_psum = sem(f"{tag}_z2_psum")
                u_made = sem(f"{tag}_u_made")
                log2_made = sem(f"{tag}_log2_made")
                gated = sem(f"{tag}_gated")
                pX, pZ = bank[0:2], bank[2:6]

            def cols_of(q):
                a, b = GROUPS[q]
                return slice(a * P, b * P), (b - a) * P

            def blocks(eng, body):
                with eng.Fori(0, NB // 2) as g:
                    for u in range(2):
                        body(2 * g + u, g, u)
                body(NB - 1, NB // 2, 0)

            with nc.Block() as block:
                @block.sync
                def _(sp):
                    def body(n, g, u):
                        if with_edges:
                            sp.wait_ge(e_used, n + 1)
                            sp.dma_start(x_e[u][:, 0:SLOTS * F], edge_v[n]).then_inc(e_in[u], 16)
                        sp.wait_ge(block_used, n + 1)
                        sp.dma_start(src_i[u][:, :], src_v[n]).then_inc(idx_in[u], 16)
                    blocks(sp, body)

                @block.gpsimd
                def _(pool):
                    def body(n, g, u):
                        pool.wait_ge(block_used, n + 1)
                        pool.wait_ge(idx_in[u], 16 * (g + 1))
                        pool.sem_inc(waited, 1)
                        for j in range(SLOTS):
                            pool.indirect_dma_start(
                                buf[u][:, j, 0:width], None, table,
                                bass.IndirectOffsetOnAxis(ap=src_i[u][:, j:j + 1], axis=0),
                            ).then_inc(gathered[u], 16)
                    blocks(pool, body)

                @block.tensor
                def _(pe):
                    pe.sem_inc(block_used, 2)
                    if with_edges:
                        pe.sem_inc(e_used, 2)
                    pe.sem_inc(hot_used[0], 1)
                    pe.sem_inc(hot_used[1], 1)

                    def transposes(n, g, u, q):
                        if q == 0:
                            pe.wait_ge(e_in[u], 16 * (g + 1))
                        a, b = GROUPS[q]
                        for k in range(a, b):
                            last = pe.transpose(pX[q % 2][:, (k - a) * P:(k - a + 1) * P],
                                                x_e[u][:, k * P:(k + 1) * P], ident[:, :])
                        last.then_inc(xT_psum, 1)
                        if q == NG - 1:
                            pe.wait_ge(xT_psum, NG * n + NG)
                            pe.sem_inc(e_used, 1)

                    def first_layer(n, g, u):
                        transposes(n, g, u, 0)
                        for q in range(NG):
                            if q + 1 < NG:
                                transposes(n, g, u, q + 1)
                            cs, w = cols_of(q)
                            pe.wait_ge(xT_made, NG * n + q + 1)
                            pe.wait_ge(u_made, NG * n + q + 1)
                            pe.matmul(pZ[q][:, 0:w], we1_2[:, :], xT_e[:, cs], start=True,
                                      stop=True).then_inc(z1_psum, 1)

                    def second_layer(n):
                        for q, (a, b) in enumerate(GROUPS):
                            pe.wait_ge(s1_made, NG * n + q + 1)
                            for k in range(a, b):
                                last = pe.matmul(pZ[q][:, (k - a) * P:(k - a + 1) * P], s1[:, k * P:(k + 1) * P],
                                                 we2_2[:, :], start=True, stop=True)
                            last.then_inc(z2_psum, 1)

                    def add_up(n, g, u):
                        if with_edges:
                            pe.wait_ge(gated, n + 1)
                        else:
                            pe.wait_ge(gathered[u], 16 * SLOTS * (g + 1))
                        since, to, _ = windows(pe, n, False)
                        with pe.Fori(since, to) as visit:
                            pe.wait_ge(acc_added, visit + 1)
                            for h, (a, b) in enumerate(HALVES):
                                pe.wait_ge(hot_made[h], visit + 1)
                                for j in range(a, b):
                                    last = pe.matmul(sums[0:cols, 0:WIN], buf[u][:, j, 0:cols],
                                                     hot[h][:, j - a, :], start=(j == 0), stop=(j == SLOTS - 1))
                                last.then_inc(hot_used[h], 1)
                        pe.drain().then_inc(block_used, 1)

                    def body(n, g, u):
                        if with_edges:
                            ahead = (n + 1, g + u, 1 - u)
                            first_layer(*ahead)
                            add_up(n, g, u)
                            second_layer(ahead[0])
                        else:
                            add_up(n, g, u)

                    if with_edges:
                        first_layer(0, 0, 0)
                        second_layer(0)
                    with pe.Fori(0, NB // 2) as g:
                        for u in range(2):
                            body(2 * g + u, g, u)
                    add_up(NB - 1, NB // 2, 0)

                if with_edges:
                    @block.scalar
                    def _(act):
                        act.preload_act_table_set("natural_log_exp_and_others")

                        def log_of(o, in_, bias, made):
                            if bias is None:
                                act.activation(o, in_, ACT.Abs)
                            else:
                                act.activation(o, in_, ACT.Abs, bias=bias)
                            act.drain()
                            act.activation(o, o, ACT.Exp, scale=-1.0)
                            act.drain()
                            act.activation(o, o, ACT.Ln, bias=1.0).then_inc(made, 1)

                        with act.Fori(0, NB) as n:
                            for q in range(NG):
                                cs, w = cols_of(q)
                                act.wait_ge(xT_psum, NG * n + q + 1)
                                act.copy(xT_e[:, cs], pX[q % 2][:, 0:w]).then_inc(xT_made, 1)
                            for q in range(NG):
                                cs, w = cols_of(q)
                                act.wait_ge(z1_psum, NG * n + q + 1)
                                log_of(lg1[:, cs], pZ[q][:, 0:w], c_be1[:, :], log1_made)
                            for q in range(NG):
                                cs, w = cols_of(q)
                                act.wait_ge(u_made, NG * n + q + NG + 1)
                                log_of(lg2[:, cs], gate_e[:, cs], None, log2_made)

                @block.vector
                def _(dve):
                    dve.sem_inc(acc_added, 1)
                    if with_edges:
                        dve.sem_inc(u_made, NG)

                    def edge_network(n):
                        for q in range(NG):
                            cs, w = cols_of(q)
                            dve.wait_ge(log1_made, NG * n + q + 1)
                            dve.scalar_tensor_tensor(s1[:, cs], pZ[q][:, 0:w], n_be1[:, :], lg1[:, cs],
                                                     ALU.max, ALU.add).then_inc(s1_made, 1)
                        for q in range(NG):
                            cs, w = cols_of(q)
                            dve.wait_ge(z2_psum, NG * n + q + 1)
                            dve.tensor_tensor(gate_e[:, cs], pZ[q][:, 0:w], be2_wide[:, 0:w],
                                              ALU.add).then_inc(u_made, 1)
                        for q in range(NG):
                            cs, w = cols_of(q)
                            dve.wait_ge(log2_made, NG * n + q + 1)
                            dve.scalar_tensor_tensor(gate_e[:, cs], gate_e[:, cs], 0.0, lg2[:, cs],
                                                     ALU.max, ALU.add)

                    def add_up(n, g, u):
                        if with_edges:
                            dve.wait_ge(gathered[u], 16 * SLOTS * (g + 1))
                            dve.sem_inc(waited, 1)
                            dve.drain()
                            h = big[:, u, :]
                            dve.scalar_tensor_tensor(h, gate_e[:, 0:SLOTS * F], -LOG2, h, ALU.add,
                                                     ALU.mult).then_inc(gated, 1)
                        since, to, first = windows(dve, n, True)
                        with dve.Fori(since, to) as visit:
                            window = nc.s_assert_within(
                                visit - since + first, 0, NW - 1,
                                skip_runtime_bounds_check_because="a visit's window is that of a dst")
                            for h, (a, b) in enumerate(HALVES):
                                dve.wait_ge(hot_used[h], visit + 1)
                                d = dst_f[:, bass.ds(n, 1), a:b].rearrange("p o j -> p (o j)")
                                dve.scalar_tensor_tensor(
                                    hot[h][:, :, :], d.unsqueeze(2).to_broadcast([P, b - a, WIN]),
                                    win_base[:, bass.ds(window, 1)],
                                    iota_row[:, :].unsqueeze(1).to_broadcast([P, b - a, WIN]),
                                    ALU.subtract, ALU.is_equal).then_inc(hot_made[h], 1)
                            dve.wait_ge(hot_used[1], visit + 2)
                            dve.wait_ge(acc_added, visit + 1)
                            a_w = acc[0:cols, bass.ds(window * WIN, WIN)]
                            dve.tensor_tensor(a_w, a_w, sums[0:cols, 0:WIN], ALU.add).then_inc(acc_added, 1)

                    def body(n, g, u):
                        add_up(n, g, u)
                        if with_edges:
                            edge_network(n + 1)

                    if with_edges:
                        edge_network(0)
                    with dve.Fori(0, NB // 2) as g:
                        for u in range(2):
                            body(2 * g + u, g, u)
                    add_up(NB - 1, NB // 2, 0)

        def wide(per_row):
            return per_row.unsqueeze(2).to_broadcast([SUB, NSUB, F])

        def norm_center(dve, y, var, var_made):
            dve.drain()
            dve.tensor_reduce(st_sum[:, :], y, AX.X, ALU.add)
            dve.drain()
            dve.tensor_scalar(st_mean[:, :], st_sum[:, :], 1.0 / F, None, ALU.mult)
            dve.drain()
            dve.tensor_tensor(y, y, wide(st_mean[:, :]), ALU.subtract)
            dve.drain()
            dve.tensor_tensor(sq[:, :, :], y, y, ALU.mult)
            dve.drain()
            dve.tensor_reduce(st_sum[:, :], sq[:, :, :], AX.X, ALU.add)
            dve.drain()
            dve.tensor_scalar(var, st_sum[:, :], 1.0 / F, EPS, ALU.mult, ALU.add).then_inc(var_made, 1)

        def inverse_root(act, o, var, made):
            act.activation(o, var, ACT.Ln)
            act.drain()
            act.activation(o, o, ACT.Exp, scale=-0.5).then_inc(made, 1)

        def chunk_loop(eng, body):
            with eng.Fori(0, NC // 2) as g:
                for b in range(2):
                    body(2 * g + b, g, b)
            body(NC - 1, NC // 2, 0)

        edge_phase("e1", p1_table, msgs, H, MSG0, False)

        b_deg_psum = sem("b_deg_psum")
        b_pre = sem("b_pre")
        b_h = sem("b_h")
        b_h_psum = sem("b_h_psum")
        b_out = sem("b_out")
        b_store = [sem(f"b_store{b}") for b in range(2)]
        with nc.Block() as block:
            @block.tensor
            def _(pe):
                def chunk(c, g, b):
                    pe.matmul(bank[0][0:P - ONES_AT, 0:CH], ident[0:MSG0, ONES_AT:P],
                              acc[0:MSG0, bass.ds(c * CH, CH)], start=True, stop=True).then_inc(b_deg_psum, 1)
                    pe.wait_ge(b_h, c + 1)
                    pe.wait_ge(b_out, c + 1)
                    pe.sem_inc(waited, 1)
                    for s in range(NSUB):
                        last = pe.transpose(bank[1][0:SUB, s * H:(s + 1) * H], nT[0:H, s * SUB:(s + 1) * SUB],
                                            ident[0:H, 0:H])
                    last.then_inc(b_h_psum, 1)
                chunk_loop(pe, chunk)

            @block.vector
            def _(dve):
                dve.sem_inc(b_out, 1)

                def chunk(c, g, b, first=False):
                    cs = bass.ds(c * CH, CH)
                    dve.wait_ge(b_deg_psum, c + 1)
                    dve.tensor_scalar(nT2[0:H, :], bank[0][0:H, 0:CH], 1.0, None, ALU.max)
                    dve.drain()
                    dve.reciprocal(inv_deg[:, :], nT2[0:H, :])
                    dve.drain()
                    dve.tensor_tensor(nT2[0:H, :], acc[0:H, cs], inv_deg[:, :], ALU.mult)
                    dve.drain()
                    dve.tensor_tensor(hT[:, cs], nT2[0:H, :], hT[:, cs], ALU.add).then_inc(b_pre, 1)
                    dve.wait_ge(b_h_psum, c + 1)
                    if not first:
                        dve.wait_ge(b_store[b], 16 * g)
                    dve.sem_inc(waited, 1)
                    dve.tensor_copy(hT[:, cs], nT[0:H, :])
                    dve.tensor_copy(o_small[b][:, :, :],
                                    bank[1][0:SUB, 0:NSUB * H].rearrange("q (s f) -> q s f", f=H)).then_inc(b_out, 1)
                chunk(0, 0, 0, True)
                chunk(1, 0, 1, True)
                with dve.Fori(1, NC // 2) as g:
                    for b in range(2):
                        chunk(2 * g + b, g, b)
                chunk(NC - 1, NC // 2, 0)

            @block.scalar
            def _(act):
                with act.Fori(0, NC) as c:
                    act.wait_ge(b_pre, c + 1)
                    act.wait_ge(b_out, c + 1)
                    act.activation(nT[0:H, :], hT[:, bass.ds(c * CH, CH)], ACT.Tanh).then_inc(b_h, 1)

            @block.sync
            def _(sp):
                def chunk(c, g, b):
                    sp.wait_ge(b_out, c + 2)
                    sp.dma_start(h1_v[c], o_small[b][:, :, :]).then_inc(b_store[b], 16)
                chunk_loop(sp, chunk)
                sp.wait_ge(b_store[0], 16 * (NC // 2 + 1))
                sp.wait_ge(b_store[1], 16 * (NC // 2))

            @block.gpsimd
            def _(pool):
                with pool.Fori(0, NC) as c:
                    pool.wait_ge(b_pre, c + 1)
                    pool.sem_inc(waited, 1)
                    pool.tensor_copy(acc[0:H, bass.ds(c * CH, CH)], zeros[0:H, :])

        edge_phase("e2", h1_table, msgs, H, H, False)

        c_deg_psum = sem("c_deg_psum")
        c_mean = sem("c_mean")
        c_o_psum = sem("c_o_psum")
        c_tanh = sem("c_tanh")
        c_var = sem("c_var")
        c_x_in = [sem(f"c_x_in{b}") for b in range(2)]
        with nc.Block() as block:
            @block.sync
            def _(sp):
                def load_x(c, b):
                    sp.dma_start(x_n[b][:, :, :], x_v[c]).then_inc(c_x_in[b], 16)

                load_x(0, 0)
                load_x(1, 1)

                with sp.Fori(0, NC // 2 - 1) as g:
                    for b in range(2):
                        sp.wait_ge(c_var, 2 * g + b + 1)
                        load_x(2 * g + b + 2, b)
                sp.wait_ge(c_var, NC - 2)
                load_x(NC - 1, 0)

            @block.vector
            def _(dve):
                def chunk(c, g, b):
                    cs = bass.ds(c * CH, CH)
                    dve.tensor_copy(h_chunk[:, :], hT[:, cs])
                    dve.wait_ge(c_deg_psum, c + 1)
                    dve.tensor_scalar(nT2[0:H, :], bank[3][0:H, 0:CH], 1.0, None, ALU.max)
                    dve.drain()
                    dve.reciprocal(inv_deg[:, :], nT2[0:H, :])
                    dve.drain()
                    dve.tensor_tensor(nT2[0:H, :], acc[0:H, cs], inv_deg[:, :], ALU.mult).then_inc(c_mean, 1)
                    dve.wait_ge(c_tanh, c + 1)
                    dve.wait_ge(c_x_in[b], 16 * (g + 1))
                    y = x1[:, bass.ds(c * NSUB, NSUB), :]
                    dve.tensor_tensor(y, yv[:, :, :], x_n[b][:, :, :], ALU.add)
                    norm_center(dve, y, x1_var[:, bass.ds(c * NSUB, NSUB)], c_var)
                chunk_loop(dve, chunk)

            @block.gpsimd
            def _(pool):
                with pool.Fori(0, NC) as c:
                    pool.wait_ge(c_mean, c + 1)
                    pool.sem_inc(waited, 1)
                    pool.tensor_copy(acc[:, bass.ds(c * CH, CH)], zeros[:, :])

            @block.scalar
            def _(act):
                with act.Fori(0, NC) as c:
                    act.wait_ge(c_o_psum, c + 1)
                    act.activation(yv[:, :, :], bank[0][0:SUB, 0:NSUB * F].rearrange("q (s f) -> q s f", f=F),
                                   ACT.Tanh).then_inc(c_tanh, 1)

            @block.tensor
            def _(pe):
                with pe.Fori(0, NC) as c:
                    pe.matmul(bank[3][0:P - ONES_AT, 0:CH], ident[0:MSG0, ONES_AT:P],
                              acc[0:MSG0, bass.ds(c * CH, CH)], start=True, stop=True).then_inc(c_deg_psum, 1)
                    pe.wait_ge(c_mean, c + 1)
                    for s in range(NSUB):
                        o = bank[0][0:SUB, s * F:(s + 1) * F]
                        pe.matmul(o, nT2[0:H, s * SUB:(s + 1) * SUB], w2a[:, :], start=True, stop=False)
                        pe.matmul(o, h_chunk[:, s * SUB:(s + 1) * SUB], w2r[:, :], start=False, stop=False)
                        last = pe.matmul(o, ones_row[:, 0:SUB], r_b2[:, :], start=False, stop=True)
                    last.then_inc(c_o_psum, 1)
                    pe.wait_ge(c_o_psum, c + 1)

        f_rstd = sem("f_rstd")
        f_x1 = sem("f_x1")
        f_xT_psum = sem("f_xT_psum")
        f_xT = sem("f_xT")
        f_hn_psum = sem("f_hn_psum")
        f_out = sem("f_out")
        f_store = [sem(f"f_store{b}") for b in range(2)]
        with nc.Block() as block:
            @block.scalar
            def _(act):
                inverse_root(act, x1_rstd[:, :], x1_var[:, :], f_rstd)

                def chunk(c, g, b, first=False):
                    act.wait_ge(f_xT_psum, c + 1)
                    act.copy(nT[:, :], bank[1][0:F, 0:CH]).then_inc(f_xT, 1)
                    act.wait_ge(f_hn_psum, c + 1)
                    if not first:
                        act.wait_ge(f_store[b], 16 * g)
                    act.copy(o_wide[b][:, :, :],
                             bank[2][0:SUB, 0:NSUB * F].rearrange("q (s f) -> q s f", f=F)).then_inc(f_out, 1)
                chunk(0, 0, 0, True)
                chunk(1, 0, 1, True)
                with act.Fori(1, NC // 2) as g:
                    for b in range(2):
                        chunk(2 * g + b, g, b)
                chunk(NC - 1, NC // 2, 0)

            @block.vector
            def _(dve):
                dve.wait_ge(f_rstd, 1)
                def chunk(c, g, b, first=False):
                    y = x1[:, bass.ds(c * NSUB, NSUB), :]
                    dve.tensor_tensor(y, y, wide(x1_rstd[:, bass.ds(c * NSUB, NSUB)]), ALU.mult)
                    dve.drain()
                    if not first:
                        dve.wait_ge(f_xT_psum, c)
                        dve.sem_inc(waited, 1)
                    dve.tensor_copy(yv[:, :, :], y).then_inc(f_x1, 1)
                chunk(0, 0, 0, True)
                with dve.Fori(1, NC) as c:
                    chunk(c, None, None)

            @block.tensor
            def _(pe):
                with pe.Fori(0, NC) as c:
                    pe.wait_ge(f_x1, c + 1)
                    pe.sem_inc(waited, 1)
                    for s in range(NSUB):
                        last = pe.transpose(bank[1][0:F, s * SUB:(s + 1) * SUB], yv[:, s, :],
                                            ident[0:SUB, 0:SUB])
                    last.then_inc(f_xT_psum, 1)
                    pe.wait_ge(f_xT, c + 1)
                    for s in range(NSUB):
                        o = bank[2][0:SUB, s * F:(s + 1) * F]
                        pe.matmul(o, nT[:, s * SUB:(s + 1) * SUB], wn[:, :], start=True, stop=False)
                        last = pe.matmul(o, ones_row[:, 0:SUB], r_bn[:, :], start=False, stop=True)
                    last.then_inc(f_hn_psum, 1)

            @block.sync
            def _(sp):
                def chunk(c, g, b):
                    sp.wait_ge(f_out, c + 1)
                    sp.dma_start(hn_v[c], o_wide[b][:, :, :]).then_inc(f_store[b], 16)
                chunk_loop(sp, chunk)
                sp.wait_ge(f_store[0], 16 * (NC // 2 + 1))
                sp.wait_ge(f_store[1], 16 * (NC // 2))

        pads = sem("pads")
        with nc.Block() as block:
            @block.gpsimd
            def _(pool):
                pool.memset(x_e[0][:, SLOTS * F:], 0.0)
                pool.memset(x_e[1][:, SLOTS * F:], 0.0).then_inc(pads, 1)

        edge_phase("e3", hn_table, rows, F, F, True)

        d_c_psum = sem("d_c_psum")
        d_log = sem("d_log")
        d_s = sem("d_s")
        d_o_psum = sem("d_o_psum")
        d_var = sem("d_var")
        d_rstd = sem("d_rstd")
        d_out = sem("d_out")
        d_store = [sem(f"d_store{b}") for b in range(2)]
        with nc.Block() as block:
            @block.tensor
            def _(pe):
                with pe.Fori(0, NC) as c:
                    pe.matmul(bank[0][:, 0:CH], wc[:, :], acc[:, bass.ds(c * CH, CH)], start=True,
                              stop=True).then_inc(d_c_psum, 1)
                    pe.wait_ge(d_s, c + 1)
                    for s in range(NSUB):
                        o = bank[1][0:SUB, s * F:(s + 1) * F]
                        pe.matmul(o, nT[:, s * SUB:(s + 1) * SUB], wp[:, :], start=True, stop=False)
                        last = pe.matmul(o, ones_row[:, 0:SUB], r_bp[:, :], start=False, stop=True)
                    last.then_inc(d_o_psum, 1)

            @block.scalar
            def _(act):
                act.preload_act_table_set("natural_log_exp_and_others")
                with act.Fori(0, NC) as c:
                    act.wait_ge(d_c_psum, c + 1)
                    act.activation(nT2[:, :], bank[0][0:F, 0:CH], ACT.Abs, bias=c_bc[:, :])
                    act.drain()
                    act.activation(nT2[:, :], nT2[:, :], ACT.Exp, scale=-1.0)
                    act.drain()
                    act.activation(nT2[:, :], nT2[:, :], ACT.Ln, bias=1.0).then_inc(d_log, 1)
                    act.wait_ge(d_var, c + 1)
                    inverse_root(act, st_rstd[:, :], st_var[:, :], d_rstd)

            @block.vector
            def _(dve):
                def chunk(c, g, b, first=False):
                    dve.wait_ge(d_log, c + 1)
                    dve.scalar_tensor_tensor(nT[:, :], bank[0][0:F, 0:CH], n_bc[:, :], nT2[:, :], ALU.max, ALU.add)
                    dve.drain()
                    dve.tensor_scalar(nT[:, :], nT[:, :], bc_off[:, :], None, ALU.add).then_inc(d_s, 1)
                    dve.wait_ge(d_o_psum, c + 1)
                    dve.tensor_tensor(yv[:, :, :], bank[1][0:SUB, 0:NSUB * F].rearrange("q (s f) -> q s f", f=F),
                                      x1[:, bass.ds(c * NSUB, NSUB), :], ALU.add)
                    norm_center(dve, yv[:, :, :], st_var[:, :], d_var)
                    dve.wait_ge(d_rstd, c + 1)
                    if not first:
                        dve.wait_ge(d_store[b], 16 * g)
                    dve.tensor_tensor(o_wide[b][:, :, :], yv[:, :, :], wide(st_rstd[:, :]),
                                      ALU.mult).then_inc(d_out, 1)
                chunk(0, 0, 0, True)
                chunk(1, 0, 1, True)
                with dve.Fori(1, NC // 2) as g:
                    for b in range(2):
                        chunk(2 * g + b, g, b)
                chunk(NC - 1, NC // 2, 0)

            @block.sync
            def _(sp):
                def chunk(c, g, b):
                    sp.wait_ge(d_out, c + 1)
                    sp.dma_start(out_v[c], o_wide[b][:, :, :]).then_inc(d_store[b], 16)
                chunk_loop(sp, chunk)
                sp.wait_ge(d_store[0], 16 * (NC // 2 + 1))
                sp.wait_ge(d_store[1], 16 * (NC // 2))


_INS = ["x", "src", "dst", "edge", "W_lin", "b_lin", "W1_agg", "W1_root", "b1", "W2_agg", "W2_root", "b2",
        "WnT", "bn", "We1T", "be1", "We2T", "be2", "WcT", "bc", "WpT", "bp"]


def kernel(x, src, dst, edge_attr_64, L0_gnn_W_lin, L0_gnn_b_lin, L0_gnn_W1_agg, L0_gnn_W1_root, L0_gnn_b1,
           L0_gnn_W2_agg, L0_gnn_W2_root, L0_gnn_b2, L1_gnn_Wn, L1_gnn_bn, L1_gnn_We1, L1_gnn_be1, L1_gnn_We2,
           L1_gnn_be2, L1_gnn_Wc, L1_gnn_bc, L1_gnn_Wp, L1_gnn_bp):
    import numpy as np
    import concourse.bacc as bacc
    from concourse.bass_utils import run_bass_kernel_spmd

    def col(a):
        return np.asarray(a).reshape(-1, 1)

    def row(a):
        return np.asarray(a).reshape(1, -1)

    def turned(a):
        return np.asarray(a).T

    values = [x, src, dst, edge_attr_64, L0_gnn_W_lin, col(L0_gnn_b_lin), L0_gnn_W1_agg, L0_gnn_W1_root,
              col(L0_gnn_b1), L0_gnn_W2_agg, L0_gnn_W2_root, row(L0_gnn_b2), turned(L1_gnn_Wn), row(L1_gnn_bn),
              turned(L1_gnn_We1), col(L1_gnn_be1), turned(L1_gnn_We2), row(L1_gnn_be2), turned(L1_gnn_Wc),
              col(L1_gnn_bc), turned(L1_gnn_Wp), row(L1_gnn_bp)]
    nc = bacc.Bacc("TRN2", target_bir_lowering=False, num_devices=1)
    arrays, args = {}, []
    for name, value in zip(_INS, values):
        a = np.ascontiguousarray(value)
        arrays[f"in_{name}"] = a
        args.append(nc.dram_tensor(f"in_{name}", a.shape, mybir.dt.from_np(a.dtype), kind="ExternalInput").ap())
    args.append(nc.dram_tensor("out_dram", (V, F), F32, kind="ExternalOutput").ap())
    gnn_kernel(nc, *args)
    result = run_bass_kernel_spmd(nc, [arrays], core_ids=[0])
    return result.results[0]["out_dram"]
```

```python
import concourse.bass as bass
import concourse.mybir as mybir
from contextlib import ExitStack

F32 = mybir.dt.float32
I32 = mybir.dt.int32
BF16 = mybir.dt.bfloat16
ALU = mybir.AluOpType
ACT = mybir.ActivationFunctionType
AX = mybir.AxisListType

P = 128
V = 12500
E = 400000
F = 64
H = 16
LOG2 = 0.6931471805599453
EPS = 1e-5

SLOTS = 25
EB = P * SLOTS
NB = E // EB
PAIRS = (SLOTS + 1) // 2
HALVES = ((0, 13), (13, SLOTS))
GROUPS = ((0, 4), (4, 7), (7, 10), (10, 13))
NG = len(GROUPS)

WIN = 128
NW = -(-V // WIN)
VP = NW * WIN

SUB = 125
NSUB = 4
CH = SUB * NSUB
NC = V // CH
assert NB * EB == E and NC * CH == V

ROW0 = 4 * H
HI, MID, ONES, LO = 0, H, 2 * H, 3 * H

SEL = 2
AUP = 25
NA = 4 * AUP
BIG = 2.0 ** 126
assert NA >= NW and AUP * H <= 512

def gnn_kernel(nc, x, src, dst, edge, W_lin, b_lin, W1_agg, W1_root, b1, W2_agg, W2_root, b2,
               WnT, bn, We1T, be1, We2T, be2, WcT, bc, WpT, bp, out):
    ctx = ExitStack()
    with ctx:
        def sb(name, shape, dt=F32):
            return ctx.enter_context(nc.sbuf_tensor(name, shape, dt))

        def pb(name, shape):
            return ctx.enter_context(nc.psum_tensor(name, shape, F32))

        def sem(name):
            return ctx.enter_context(nc.semaphore(name))

        p1_table = nc.dram_tensor("p1_table", (V, ROW0), BF16).ap()
        h1_table = nc.dram_tensor("h1_table", (V, ROW0), BF16).ap()
        hn_table = nc.dram_tensor("hn_table", (V, F), F32).ap()
        deg_dram = nc.dram_tensor("deg_dram", (2, VP), F32).ap()

        sel_dram = nc.dram_tensor("sel_dram", (NB, 2 * SEL * P), BF16).ap()

        src_v = src.rearrange("(n p j) -> n p j", p=P, j=SLOTS)
        dst_v = dst.rearrange("(n p j) -> p n j", p=P, j=SLOTS)
        edge_v = edge.rearrange("(n p j) f -> n p (j f)", p=P, j=SLOTS)

        def chunks(t):
            return t.rearrange("(c s q) f -> c q s f", s=NSUB, q=SUB)

        out_v = chunks(out)
        x_all = x.rearrange("(t q) f -> q t f", q=SUB)
        X_PARTS = 5
        X_TILES = NC * NSUB // X_PARTS
        p1_v, h1_v, hn_v = chunks(p1_table), chunks(h1_table), chunks(hn_table)

        ident = sb("ident", [P, P])
        iota_i = sb("iota_i", [P, P], I32)
        iota_row = sb("iota_row", [P, WIN])
        win_base_i = sb("win_base_i", [P, NW + 1], I32)
        win_base = sb("win_base", [P, NW + 1])
        upto = sb("upto", [P, P])
        zeros = sb("zeros", [F, CH])
        add_parts = sb("add_parts", [ROW0, P])
        ones_row = sb("ones_row", [1, P])
        ones_blk = sb("ones_blk", [F, P])

        w_lin = sb("w_lin", [F, F])
        w1a = sb("w1a", [F, H])
        w1r = sb("w1r", [F, H])
        w2a = sb("w2a", [H, F])
        w2r = sb("w2r", [H, F])
        wn = sb("wn", [F, F])
        wc = sb("wc", [F, 2 * F])
        wp = sb("wp", [F, F])
        we2 = sb("we2", [F, F])
        we1_2 = sb("we1_2", [P, P])
        we2_2 = sb("we2_2", [P, P])
        c_lin = sb("c_lin", [F, 1])
        c_b1 = sb("c_b1", [H, 1])
        c_be1 = sb("c_be1", [P, 1])
        n_be1 = sb("n_be1", [P, 1])
        c_bc = sb("c_bc", [F, 1])
        n_bc = sb("n_bc", [F, 1])
        bc_off = sb("bc_off", [F, 1])
        be1_off = sb("be1_off", [F, 1])
        be1_wide = sb("be1_wide", [F, P])
        r_b2 = sb("r_b2", [1, F])
        r_bn = sb("r_bn", [1, F])
        r_be2 = sb("r_be2", [1, F])
        r_bp = sb("r_bp", [1, F])
        be2_wide = sb("be2_wide", [P, 8 * F])

        dst_f = sb("dst_f", [P, NB, SLOTS])
        dst_ext = sb("dst_ext", [P, 2, NB])
        ext_t = sb("ext_t", [NB, 2])
        ext_i = sb("ext_i", [NB, 2], I32)
        win_lo = sb("win_lo", [NB, 1])
        win_hi = sb("win_hi", [NB, 1])
        win_n = sb("win_n", [NB, 1])
        win_row = sb("win_row", [1, NB])
        visits = sb("visits", [1, 3 * NB], I32)

        src_i = [sb(f"src_i{u}", [P, SLOTS], I32) for u in range(2)]
        hot = [sb(f"hot{h}", [P, b - a, WIN]) for h, (a, b) in enumerate(HALVES)]
        big = sb("big", [P, 2, SLOTS * F])
        rows = [big[:, u, :].rearrange("p (j f) -> p j f", f=F) for u in range(2)]
        msgs = [big[:, u, :].bitcast(BF16)[:, 0:SLOTS * ROW0].rearrange("p (j f) -> p j f", f=ROW0)
                for u in range(2)]
        hot0 = [hot[h][:, :, :].rearrange("p j w -> p (j w)").bitcast(BF16)[:, 0:(b - a) * WIN]
                .rearrange("p (j w) -> p j w", w=WIN) for h, (a, b) in enumerate(HALVES)]

        node_col = sb("node_col", [P, 1])
        node_col_i = sb("node_col_i", [P, 1], I32)
        others = sb("others", [NA, NA, H], BF16)
        work = sb("work", [P, NA * ROW0 // 2])
        table0 = work[:, :].bitcast(BF16).rearrange("p (a c) -> p a c", c=ROW0)
        sel_in = [sb(f"sel_in{u}", [P, 2, SEL * P], BF16) for u in range(2)]
        sel_hot = sb("sel_hot", [P, 2, SEL * P], BF16)
        part_max = sb("part_max", [P, SEL, 2, H])
        rest = sb("rest", [P, SEL, H])
        picked = sb("picked", [P, SEL, H])

        acc = sb("acc", [F, VP])
        shared = sb("shared", [P, V])
        hT = shared[0:H, :]
        inv_rows = shared[2 * H:3 * H, :]
        XE = (SLOTS + 1) * F
        x_e = [shared[:, u * XE:(u + 1) * XE] for u in range(2)]
        xT_e, lg1, s1, gate_e, lg2 = (shared[:, k * XE:(k + 1) * XE] for k in range(2, 7))
        x1 = sb("x1", [SUB, NC * NSUB, F])

        CW = NSUB * F
        x_n = [sb(f"x_n{b}", [SUB, NSUB, F]) for b in range(2)]
        nT = [work[0:F, b * CH:(b + 1) * CH] for b in range(2)]
        nT2 = [work[0:F, (2 + b) * CH:(3 + b) * CH] for b in range(2)]
        h_chunk = [work[0:H, (4 + b) * CH:(5 + b) * CH] for b in range(2)]
        assert 6 * CH <= NA * ROW0 // 2
        inv_deg = sb("inv_deg", [H, CH])
        deg_wide = sb("deg_wide", [P, NW])
        o_small = [sb(f"o_small{b}", [SUB, NSUB, ROW0], BF16) for b in range(2)]
        o_rest = sb("o_rest", [SUB, NSUB, H])
        o_wide = [big[0:SUB, 0, k * CW:(k + 1) * CW].rearrange("q (s f) -> q s f", f=F) for k in (0, 1)]
        yv = [big[0:SUB, 0, k * CW:(k + 1) * CW].rearrange("q (s f) -> q s f", f=F) for k in (2, 3)]
        sq = big[0:SUB, 0, 4 * CW:5 * CW].rearrange("q (s f) -> q s f", f=F)
        st_sum = sb("st_sum", [SUB, NSUB])
        st_mean = sb("st_mean", [SUB, NSUB])
        st_var = [sb(f"st_var{b}", [SUB, NSUB]) for b in range(2)]
        st_rstd = [sb(f"st_rstd{b}", [SUB, NSUB]) for b in range(2)]
        x1_var = sb("x1_var", [SUB, NC * NSUB])
        x1_rstd = sb("x1_rstd", [SUB, NC * NSUB])

        banks = pb("banks", [P, 8 * 512])
        bank = [banks[:, i * 512:(i + 1) * 512] for i in range(8)]

        waited = sem("waited")

        weights_in = sem("weights_in")
        dst_in = sem("dst_in")
        iotas = sem("iotas")
        consts = sem("consts")
        small = sem("small")
        sel_src_in = sem("sel_src_in")
        sel_digits = sem("sel_digits")
        sel_turned = sem("sel_turned")
        sel_rows = sem("sel_rows")
        sel_out = sem("sel_out")
        ext_psum = sem("ext_psum")
        ext_sb = sem("ext_sb")
        visit_psum = sem("visit_psum")
        be2_psum = sem("be2_psum")
        setup_done = sem("setup_done")
        a_x_in = sem("a_x_in")
        a_x_chunk = sem("a_x_chunk")
        a_xT_psum = sem("a_xT_psum")
        a_xT = sem("a_xT")
        a_h_psum = sem("a_h_psum")
        a_h = sem("a_h")
        a_p_psum = sem("a_p_psum")
        a_out = sem("a_out")
        a_root = sem("a_root")
        a_store = [sem(f"a_store{b}") for b in range(2)]

        loads = [(w_lin[:, :], W_lin), (w1a[:, :], W1_agg), (w1r[:, :], W1_root), (w2a[:, :], W2_agg),
                 (w2r[:, :], W2_root), (wn[:, :], WnT), (wc[:, 0:F], WcT), (wc[:, F:2 * F], WcT), (wp[:, :], WpT), (we2[:, :], We2T),
                 (c_lin[:, :], b_lin), (c_b1[:, :], b1), (c_bc[:, :], bc),
                 (c_be1[0:F, :], be1), (c_be1[F:P, :], be1),
                 (r_b2[:, :], b2), (r_bn[:, :], bn), (r_be2[:, :], be2), (r_bp[:, :], bp)]
        corners = [(we1_2[0:F, 0:F], We1T), (we1_2[F:P, F:P], We1T),
                   (we2_2[0:F, 0:F], We2T), (we2_2[F:P, F:P], We2T)]
        ALL_IN = 16 * (len(loads) + len(corners))

        def chunks_of(eng, *stages):
            lags = [lag for _, lag in stages]
            since = 2 * -(-(max(lags) + 2) // 2)
            to = NC - NC % 2

            def step(t, g=None):
                for stage, lag in stages:
                    if g is None and not 0 <= t - lag < NC:
                        continue
                    if g is None:
                        stage(t - lag, (t - lag) // 2, (t - lag) % 2)
                    else:
                        stage(2 * g + (t - lag), g + (t - lag) // 2, (t - lag) % 2)

            for t in range(since):
                step(t)
            with eng.Fori(since // 2, to // 2) as g:
                for b in range(2):
                    step(b, g)
            for t in range(to, NC + max(lags)):
                step(t)

        def later(c):
            return not isinstance(c, int) or c >= 2

        def wait_chunk(eng, signal, c):
            eng.wait_ge(signal, c + 1)

        def wait_freed(eng, signal, c):
            if later(c):
                eng.wait_ge(signal, c - 1)

        def wait_stored(eng, stores, c, g, b):
            if later(c):
                eng.wait_ge(stores[b], 16 * g)

        def all_stored(eng, stores):
            eng.wait_ge(stores[0], 16 * (NC - NC // 2))
            eng.wait_ge(stores[1], 16 * (NC // 2))

        def table_rows(dve, o, ps, made):
            v = ps[0:SUB, 0:NSUB * H].rearrange("q (s f) -> q s f", f=H)
            dve.tensor_copy(o[:, :, HI:HI + H], v)
            dve.drain()
            dve.tensor_tensor(o_rest[:, :, :], v, o[:, :, HI:HI + H], ALU.subtract)
            dve.drain()
            dve.tensor_copy(o[:, :, MID:MID + H], o_rest[:, :, :])
            dve.drain()
            dve.tensor_tensor(o[:, :, LO:LO + H], o_rest[:, :, :], o[:, :, MID:MID + H],
                              ALU.subtract).then_inc(made, 1)

        def features(ps):
            return ps[0:SUB, 0:NSUB * F].rearrange("q (s f) -> q s f", f=F)

        SB = SEL * NB
        sel_src = big[:, 0, 0:SB].bitcast(I32).rearrange("p (n j) -> p n j", j=SEL)
        sel_digit_i = big[:, 0, SB:2 * SB].bitcast(I32)
        sel_digit = [big[:, 1, d * SB:(d + 1) * SB].rearrange("p (j n) -> p j n", n=NB) for d in range(2)]
        sel_row = hot[0][:, :, :].rearrange("p j w -> p (j w)").bitcast(BF16)[0:NB, 0:2 * SEL * P]
        assert 2 * SB <= SLOTS * F

        with nc.Block() as block:
            @block.sync
            def _(sp):
                for k in range(X_PARTS):
                    sp.dma_start(x1[:, k * X_TILES:(k + 1) * X_TILES, :],
                                 x_all[:, k * X_TILES:(k + 1) * X_TILES, :]).then_inc(a_x_in, 16)
                    if k == 0:
                        sp.dma_start(dst_f[:, :, :].bitcast(I32), dst_v).then_inc(dst_in, 16)
                        sp.dma_start(sel_src, src.rearrange("(n p j) -> p n j", p=P, j=SLOTS)
                                     [:, :, SLOTS - SEL:]).then_inc(sel_src_in, 16)

                def store_p1(c, g, b):
                    wait_chunk(sp, a_out, c)
                    sp.dma_start(p1_v[c], o_small[b][:, :, :]).then_inc(a_store[b], 16)

                chunks_of(sp, (store_p1, 0))
                sp.wait_ge(sel_rows, 1)
                sp.dma_start(sel_dram, sel_row).then_inc(sel_out, 16)
                sp.wait_ge(sel_out, 16)
                all_stored(sp, a_store)

            @block.gpsimd
            def _(pool):
                pool.memset(ident[:, :], 0.0)
                pool.memset(upto[:, :], 1.0)
                pool.memset(zeros[:, :], 0.0)
                pool.memset(ones_row[:, :], 1.0)
                pool.memset(ones_blk[:, :], 1.0)
                pool.memset(we1_2[:, :], 0.0)
                pool.memset(we2_2[:, :], 0.0)
                pool.iota(node_col_i[:, :], pattern=[[0, 1]], base=0, channel_multiplier=1)
                pool.iota(iota_i[:, :], pattern=[[1, WIN]], base=0, channel_multiplier=0)
                pool.iota(win_base_i[:, :], pattern=[[WIN, NW + 1]], base=0, channel_multiplier=0).then_inc(iotas, 1)
                pool.wait_ge(iotas, 1)
                pool.affine_select(out=ident[:, :], in_=ident[:, :], compare_op=ALU.not_equal, fill=1.0,
                                   base=0, pattern=[[-1, P]], channel_multiplier=1)
                pool.affine_select(out=upto[:, :], in_=upto[:, :], compare_op=ALU.is_ge, fill=0.0,
                                   base=0, pattern=[[1, P]], channel_multiplier=-1)
                pool.memset(add_parts[:, :], 0.0)
                pool.memset(acc[:, :], 0.0)
                pool.memset(others[:, :, :], -BIG)
                for b in range(2):
                    pool.memset(o_small[b][:, :, ONES:LO], 1.0)
                pool.drain().then_inc(iotas, 1)
                pool.wait_ge(iotas, 2)
                for part in (HI, MID, LO):
                    pool.affine_select(out=add_parts[:, 0:H], in_=add_parts[:, 0:H], compare_op=ALU.not_equal,
                                       fill=1.0, base=-part, pattern=[[-1, H]], channel_multiplier=1)
                    pool.drain()
                pool.affine_select(out=others[:, :, :], in_=others[:, :, :], compare_op=ALU.not_equal,
                                   fill=0.0, base=0, pattern=[[-1, NA], [0, H]],
                                   channel_multiplier=1).then_inc(consts, 1)

                def x_chunk(c, g, b):
                    wait_freed(pool, a_xT_psum, c)
                    if later(c):
                        pool.sem_inc(waited, 1)
                    pool.tensor_copy(x_n[b][:, :, :], x1[:, bass.ds(c * NSUB, NSUB), :]).then_inc(a_x_chunk, 1)

                pool.wait_ge(a_x_in, 16 * X_PARTS)
                chunks_of(pool, (x_chunk, 0))

            @block.scalar
            def _(act):
                for tile, dram in loads:
                    act.dma_start(tile, dram).then_inc(weights_in, 16)
                act.wait_ge(iotas, 1)
                for tile, dram in corners:
                    act.dma_start(tile, dram).then_inc(weights_in, 16)
                act.wait_ge(weights_in, ALL_IN)

                def x_turned(c, g, b):
                    wait_chunk(act, a_xT_psum, c)
                    act.copy(nT[b][:, :], bank[b][0:F, 0:CH]).then_inc(a_xT, 1)

                def h0(c, g, b):
                    wait_chunk(act, a_h_psum, c)
                    wait_freed(act, a_p_psum, c)
                    act.activation(nT2[b][:, :], bank[2 + b][0:F, 0:CH], ACT.Identity,
                                   bias=c_lin[:, :]).then_inc(a_h, 1)

                chunks_of(act, (x_turned, 0), (h0, 1))
                act.wait_ge(sel_turned, 1)
                for k in range(0, 2 * SEL, 4):
                    last = act.copy(sel_row[:, k * P:(k + 4) * P], bank[k // 4][0:NB, :])
                last.then_inc(sel_rows, 1)

            @block.tensor
            def _(pe):
                pe.wait_ge(consts, 1)
                pe.wait_ge(weights_in, ALL_IN)

                def turn_x(c, g, b):
                    wait_chunk(pe, a_x_chunk, c)
                    pe.sem_inc(waited, 1)
                    for s in range(NSUB):
                        last = pe.transpose(bank[b][0:F, s * SUB:(s + 1) * SUB], x_n[b][:, s, :],
                                            ident[0:SUB, 0:SUB])
                    last.then_inc(a_xT_psum, 1)

                def h0(c, g, b):
                    wait_chunk(pe, a_xT, c)
                    pe.sem_inc(waited, 1)
                    pe.matmul(bank[2 + b][0:F, 0:CH], w_lin[:, :], nT[b][:, :], start=True,
                              stop=True).then_inc(a_h_psum, 1)

                def products(c, g, b):
                    wait_chunk(pe, a_h, c)
                    wait_freed(pe, a_out, c)
                    pe.sem_inc(waited, 1)
                    for s in range(NSUB):
                        pe.matmul(bank[4 + b][0:SUB, s * H:(s + 1) * H], nT2[b][:, s * SUB:(s + 1) * SUB],
                                  w1a[:, :], start=True, stop=True)
                    pe.matmul(bank[6 + b][0:H, 0:CH], w1r[:, :], nT2[b][:, :], start=True,
                              stop=True).then_inc(a_p_psum, 1)

                chunks_of(pe, (turn_x, 0), (h0, 1), (products, 2))
                pe.wait_ge(a_out, NC)
                pe.wait_ge(sel_digits, 1)
                for k in range(2 * SEL):
                    last = pe.transpose(bank[k // 4][0:NB, (k % 4) * P:(k % 4 + 1) * P],
                                        sel_digit[k // SEL][:, k % SEL, :], ident[:, :])
                last.then_inc(sel_turned, 1)
                pe.wait_ge(a_out, NC)
                pe.wait_ge(small, 1)
                for k in range(2):
                    last = pe.transpose(bank[4][0:NB, k * P:(k + 1) * P], dst_ext[:, k, :], ident[:, :])
                last.then_inc(ext_psum, 1)
                pe.wait_ge(ext_sb, 1)
                pe.matmul(bank[5][0:1, 0:NB], win_n[:, :], upto[0:NB, 0:NB], start=True, stop=True)
                pe.matmul(bank[5][0:1, NB:2 * NB], win_n[:, :], ident[0:NB, 0:NB], start=True, stop=True)
                pe.matmul(bank[5][0:1, 2 * NB:3 * NB], win_lo[:, :], ident[0:NB, 0:NB], start=True,
                          stop=True).then_inc(visit_psum, 1)
                pe.matmul(bank[6][:, 0:F], be1_wide[:, :], we2[:, :], start=True, stop=False)
                pe.matmul(bank[6][:, 0:F], ones_row[:, :], r_be2[:, :], start=False,
                          stop=True).then_inc(be2_psum, 1)

            @block.vector
            def _(dve):
                dve.wait_ge(iotas, 1)
                dve.tensor_copy(iota_row[:, :], iota_i[:, :])
                dve.tensor_copy(win_base[:, :], win_base_i[:, :])
                dve.tensor_copy(node_col[:, :], node_col_i[:, :])
                dve.wait_ge(weights_in, ALL_IN)
                dve.wait_ge(consts, 1)
                dve.tensor_scalar(n_be1[:, :], c_be1[:, :], -1.0, None, ALU.mult)
                dve.tensor_scalar(n_bc[:, :], c_bc[:, :], -1.0, None, ALU.mult)
                dve.tensor_scalar(bc_off[:, :], c_bc[:, :], -LOG2, None, ALU.add)
                dve.tensor_scalar(be1_off[:, :], c_be1[0:F, :], -LOG2, None, ALU.add)
                dve.drain()
                dve.tensor_scalar(be1_wide[:, :], ones_blk[:, :], be1_off[:, :], None, ALU.mult)

                dve.wait_ge(dst_in, 16)
                dve.tensor_copy(dst_f[:, :, :], dst_f[:, :, :].bitcast(I32))
                dve.drain()
                dve.tensor_reduce(dst_ext[:, 0, :], dst_f[:, :, :], AX.X, ALU.min)
                dve.tensor_reduce(dst_ext[:, 1, :], dst_f[:, :, :], AX.X, ALU.max).then_inc(small, 1)
                dve.wait_ge(sel_src_in, 16)
                for d, (op, by) in enumerate(((ALU.bitwise_and, P - 1),
                                              (ALU.arith_shift_right, P.bit_length() - 1))):
                    dve.tensor_single_scalar(sel_digit_i, sel_src.rearrange("p n j -> p (n j)"), by, op)
                    dve.drain()
                    last = dve.tensor_copy(sel_digit[d], sel_digit_i.rearrange("p (n j) -> p j n", j=SEL))
                    dve.drain()
                dve.sem_inc(sel_digits, 1)

                def out_p1(c, g, b):
                    wait_chunk(dve, a_p_psum, c)
                    wait_stored(dve, a_store, c, g, b)
                    dve.tensor_scalar(hT[:, bass.ds(c * CH, CH)], bank[6 + b][0:H, 0:CH], c_b1[:, :], None, ALU.add)
                    table_rows(dve, o_small[b], bank[4 + b], a_out)

                chunks_of(dve, (out_p1, 0))

                dve.wait_ge(ext_psum, 1)
                dve.tensor_reduce(ext_t[:, 0:1], bank[4][0:NB, 0:P], AX.X, ALU.min)
                dve.tensor_reduce(ext_t[:, 1:2], bank[4][0:NB, P:2 * P], AX.X, ALU.max)
                dve.drain()
                dve.tensor_copy(ext_i[:, :], ext_t[:, :])
                dve.drain()
                dve.tensor_single_scalar(ext_i[:, :], ext_i[:, :], WIN.bit_length() - 1, ALU.arith_shift_right)
                dve.drain()
                dve.tensor_copy(win_lo[:, :], ext_i[:, 0:1])
                dve.tensor_copy(win_hi[:, :], ext_i[:, 1:2])
                dve.drain()
                dve.scalar_tensor_tensor(win_n[:, :], win_hi[:, :], 1.0, win_lo[:, :], ALU.add,
                                         ALU.subtract).then_inc(ext_sb, 1)
                dve.wait_ge(visit_psum, 1)
                dve.tensor_copy(win_row[:, :], bank[5][0:1, NB:2 * NB])
                dve.tensor_copy(visits[:, NB:2 * NB], bank[5][0:1, 0:NB])
                dve.tensor_copy(visits[:, 2 * NB:3 * NB], bank[5][0:1, 2 * NB:3 * NB])
                dve.drain()
                dve.tensor_tensor(visits[:, 0:NB], bank[5][0:1, 0:NB], win_row[:, :], ALU.subtract)
                dve.wait_ge(be2_psum, 1)
                for k in range(8):
                    dve.tensor_copy(be2_wide[:, k * F:(k + 1) * F], bank[6][:, 0:F])

        def windows(eng, n, with_first):
            since = eng.value_load(visits[0:1, bass.ds(n, 1)], min_val=0, max_val=NB * NW - 1)
            to = eng.value_load(visits[0:1, bass.ds(n + NB, 1)], min_val=1, max_val=NB * NW)
            if not with_first:
                return since, to, None
            first = eng.value_load(visits[0:1, bass.ds(n + 2 * NB, 1)], min_val=0, max_val=NW - 1)
            return since, to, first

        def edge_phase(tag, table, buf, hots, width, cols, with_edges):
            idx_in = [sem(f"{tag}_idx_in{u}") for u in range(2)]
            gathered = [sem(f"{tag}_gathered{u}") for u in range(2)]
            block_used = sem(f"{tag}_block_used")
            hot_made = [sem(f"{tag}_hot_made{h}") for h in range(2)]
            hot_used = [sem(f"{tag}_hot_used{h}") for h in range(2)]
            acc_added = sem(f"{tag}_acc_added")
            sums = bank[7]
            took = SLOTS if with_edges else SLOTS - SEL
            if not with_edges:
                table_in = sem(f"{tag}_table_in")
                table_tail = sem(f"{tag}_table_tail")
                sel_read = [sem(f"{tag}_sel_read{u}") for u in range(2)]
                sel_made = sem(f"{tag}_sel_made")
                sel_psum = sem(f"{tag}_sel_psum")
                sel_taken = sem(f"{tag}_sel_taken")
                msgs_made = sem(f"{tag}_msgs_made")
            if with_edges:
                e_in = [sem(f"{tag}_e_in{u}") for u in range(2)]
                e_used = sem(f"{tag}_e_used")
                xT_psum = sem(f"{tag}_xT_psum")
                xT_made = sem(f"{tag}_xT_made")
                z1_psum = sem(f"{tag}_z1_psum")
                log1_made = sem(f"{tag}_log1_made")
                s1_made = sem(f"{tag}_s1_made")
                z2_psum = sem(f"{tag}_z2_psum")
                u_made = sem(f"{tag}_u_made")
                log2_made = sem(f"{tag}_log2_made")
                gated = sem(f"{tag}_gated")
                pX, pZ = bank[0:2], bank[2:6]

            def cols_of(q):
                a, b = GROUPS[q]
                return slice(a * P, b * P), (b - a) * P

            def blocks(eng, body):
                with eng.Fori(0, NB // 2) as g:
                    for u in range(2):
                        body(2 * g + u, g, u)
                body(NB - 1, NB // 2, 0)

            with nc.Block() as block:
                @block.sync
                def _(sp):
                    if not with_edges:
                        whole = V // P
                        sp.wait_ge(table_tail, 1)
                        sp.dma_start(table0[:, 0:whole, :],
                                     table[0:whole * P, :].rearrange("(a p) c -> p a c", p=P)).then_inc(table_in, 16)
                        sp.dma_start(table0[0:V - whole * P, whole, :],
                                     table[whole * P:V, :]).then_inc(table_in, 16)

                    def body(n, g, u, last=False):
                        if with_edges:
                            if not last:
                                sp.wait_ge(e_used, n + 3)
                                sp.dma_start(x_e[u][:, 0:SLOTS * F], edge_v[n + 2]).then_inc(e_in[u], 16)
                        else:
                            sp.wait_ge(sel_made, n + 1)
                            sp.dma_start(sel_in[u][:, :, :].rearrange("p d e -> p (d e)"),
                                         sel_dram[bass.ds(n, 1), :].to_broadcast([P, 2 * SEL * P])
                                         ).then_inc(sel_read[u], 16)
                        sp.wait_ge(block_used, n + 1)
                        sp.dma_start(src_i[u][:, :], src_v[n]).then_inc(idx_in[u], 16)
                    if with_edges:
                        for u in range(2):
                            sp.wait_ge(e_used, u + 1)
                            sp.dma_start(x_e[u][:, 0:SLOTS * F], edge_v[u]).then_inc(e_in[u], 16)
                    with sp.Fori(0, NB // 2 - 1) as g:
                        for u in range(2):
                            body(2 * g + u, g, u)
                    body(NB - 3, NB // 2 - 1, 0)
                    body(NB - 2, NB // 2 - 1, 1, last=True)
                    body(NB - 1, NB // 2, 0, last=True)

                @block.gpsimd
                def _(pool):
                    def body(n, g, u):
                        pool.wait_ge(block_used, n + 1)
                        pool.wait_ge(idx_in[u], 16 * (g + 1))
                        pool.sem_inc(waited, 1)
                        for j in range(took):
                            pool.indirect_dma_start(
                                buf[u][:, j, 0:width], None, table,
                                bass.IndirectOffsetOnAxis(ap=src_i[u][:, j:j + 1], axis=0),
                            ).then_inc(gathered[u], 16)
                    blocks(pool, body)

                @block.tensor
                def _(pe):
                    pe.sem_inc(block_used, 2)
                    if with_edges:
                        pe.sem_inc(e_used, 2)
                    pe.sem_inc(hot_used[0], 1)
                    pe.sem_inc(hot_used[1], 1)

                    def transposes(n, g, u, q):
                        if q == 0:
                            pe.wait_ge(e_in[u], 16 * (g + 1))
                        a, b = GROUPS[q]
                        for k in range(a, b):
                            last = pe.transpose(pX[q % 2][:, (k - a) * P:(k - a + 1) * P],
                                                x_e[u][:, k * P:(k + 1) * P], ident[:, :])
                        last.then_inc(xT_psum, 1)
                        if q == NG - 1:
                            pe.wait_ge(xT_psum, NG * n + NG)
                            pe.sem_inc(e_used, 1)

                    def first_layer(n, g, u):
                        transposes(n, g, u, 0)
                        for q in range(NG):
                            if q + 1 < NG:
                                transposes(n, g, u, q + 1)
                            cs, w = cols_of(q)
                            pe.wait_ge(xT_made, NG * n + q + 1)
                            pe.wait_ge(u_made, NG * n + q + 1)
                            pe.matmul(pZ[q][:, 0:w], we1_2[:, :], xT_e[:, cs], start=True,
                                      stop=True).then_inc(z1_psum, 1)

                    def second_layer(n):
                        for q, (a, b) in enumerate(GROUPS):
                            pe.wait_ge(s1_made, NG * n + q + 1)
                            for k in range(a, b):
                                last = pe.matmul(pZ[q][:, (k - a) * P:(k - a + 1) * P], s1[:, k * P:(k + 1) * P],
                                                 we2_2[:, :], start=True, stop=True)
                            last.then_inc(z2_psum, 1)

                    def add_up(n, g, u):
                        since, to, _ = windows(pe, n, False)
                        if with_edges:
                            pe.wait_ge(gated, n + 1)
                        else:
                            pe.wait_ge(gathered[u], 16 * took * (g + 1))
                            pe.wait_ge(msgs_made, n + 1)
                        pe.sem_inc(waited, 1)
                        with pe.Fori(since, to) as visit:
                            pe.wait_ge(acc_added, visit + 1)
                            for h, (a, b) in enumerate(HALVES):
                                pe.wait_ge(hot_made[h], visit + 1 + (n if h == 0 else 0))
                                for j in range(a, b):
                                    last = pe.matmul(sums[0:cols, 0:WIN], buf[u][:, j, 0:cols],
                                                     hots[h][:, j - a, :], start=(j == 0), stop=(j == SLOTS - 1))
                                last.then_inc(hot_used[h], 1)
                        pe.drain().then_inc(block_used, 1)

                    def pick(n):
                        pe.wait_ge(sel_made, n + 3)
                        for k in range(SEL):
                            e = slice(k * P, (k + 1) * P)
                            for half in range(2):
                                t = 2 * k + half
                                pe.wait_ge(sel_taken, 2 * SEL * n + t + 1)
                                for i in range(2):
                                    o = bank[2 * (t % 2) + i][:, 0:AUP * H]
                                    aa = slice((2 * half + i) * AUP, (2 * half + i + 1) * AUP)
                                    for m, part in enumerate((HI, MID, LO)):
                                        pe.matmul(o, sel_hot[:, 0, e], table0[:, aa, part:part + H],
                                                  start=(m == 0), stop=False)
                                    last = pe.matmul(o, sel_hot[0:NA, 1, e], others[:, aa, :], start=False,
                                                     stop=True)
                                last.then_inc(sel_psum, 1)

                    def body(n, g, u, last=False):
                        if with_edges:
                            second_layer(n + 1)
                            if not last:
                                first_layer(n + 2, g + 1, u)
                        else:
                            pick(n + 1)
                        add_up(n, g, u)

                    if with_edges:
                        first_layer(0, 0, 0)
                        second_layer(0)
                        first_layer(1, 0, 1)
                    else:
                        pe.wait_ge(table_in, 32)
                        pick(0)
                    with pe.Fori(0, NB // 2 - 1) as g:
                        for u in range(2):
                            body(2 * g + u, g, u)
                    body(NB - 3, NB // 2 - 1, 0)
                    body(NB - 2, NB // 2 - 1, 1, last=True)
                    add_up(NB - 1, NB // 2, 0)

                if with_edges:
                    @block.scalar
                    def _(act):
                        act.preload_act_table_set("natural_log_exp_and_others")

                        def log_of(o, in_, bias, made):
                            if bias is None:
                                act.activation(o, in_, ACT.Abs)
                            else:
                                act.activation(o, in_, ACT.Abs, bias=bias)
                            act.drain()
                            act.activation(o, o, ACT.Exp, scale=-1.0)
                            act.drain()
                            act.activation(o, o, ACT.Ln, bias=1.0).then_inc(made, 1)

                        def copies(n):
                            for q in range(NG):
                                cs, w = cols_of(q)
                                act.wait_ge(xT_psum, NG * n + q + 1)
                                act.copy(xT_e[:, cs], pX[q % 2][:, 0:w]).then_inc(xT_made, 1)

                        def first_logs(n):
                            for q in range(NG):
                                cs, w = cols_of(q)
                                act.wait_ge(z1_psum, NG * n + q + 1)
                                log_of(lg1[:, cs], pZ[q][:, 0:w], c_be1[:, :], log1_made)

                        def second_logs(n):
                            for q in range(NG):
                                cs, w = cols_of(q)
                                act.wait_ge(u_made, NG * n + q + NG + 1)
                                log_of(lg2[:, cs], gate_e[:, cs], None, log2_made)

                        copies(0)
                        first_logs(0)
                        with act.Fori(0, NB - 1) as n:
                            copies(n + 1)
                            second_logs(n)
                            first_logs(n + 1)
                        second_logs(NB - 1)

                @block.vector
                def _(dve):
                    dve.sem_inc(acc_added, 1)
                    if with_edges:
                        dve.sem_inc(u_made, NG)

                    def digit_hots(n, g, u):
                        dve.wait_ge(sel_read[u], 16 * (g + 1))
                        for d in range(2):
                            last = dve.tensor_scalar(sel_hot[:, d, :], sel_in[u][:, d, :], node_col[:, :], None,
                                                     ALU.is_equal)
                        last.then_inc(sel_made, 1)

                    def pick(n, u):
                        for k in range(SEL):
                            for half in range(2):
                                t = 2 * k + half
                                dve.wait_ge(sel_psum, 2 * SEL * n + t + 1)
                                pair = banks[:, (t % 2) * 1024:(t % 2 + 1) * 1024].rearrange(
                                    "p (i c) -> p i c", i=2)[:, :, 0:AUP * H].rearrange(
                                    "p i (a f) -> p f i a", f=H)
                                dve.tensor_reduce(part_max[:, k, half, :], pair, AX.XY,
                                                  ALU.max).then_inc(sel_taken, 1)
                        dve.drain()
                        dve.tensor_tensor(picked[:, :, :], part_max[:, :, 0, :], part_max[:, :, 1, :], ALU.max)
                        dve.drain()
                        o = msgs[u][:, SLOTS - SEL:, :]
                        dve.tensor_copy(o[:, :, HI:HI + H], picked[:, :, :])
                        dve.drain()
                        dve.tensor_tensor(rest[:, :, :], picked[:, :, :], o[:, :, HI:HI + H], ALU.subtract)
                        dve.drain()
                        dve.tensor_copy(o[:, :, MID:MID + H], rest[:, :, :])
                        dve.drain()
                        dve.tensor_tensor(o[:, :, LO:LO + H], rest[:, :, :], o[:, :, MID:MID + H],
                                          ALU.subtract).then_inc(msgs_made, 1)

                    def first_activation(n):
                        for q in range(NG):
                            cs, w = cols_of(q)
                            dve.wait_ge(log1_made, NG * n + q + 1)
                            dve.scalar_tensor_tensor(s1[:, cs], pZ[q][:, 0:w], n_be1[:, :], lg1[:, cs],
                                                     ALU.max, ALU.add).then_inc(s1_made, 1)

                    def second_values(n):
                        for q in range(NG):
                            cs, w = cols_of(q)
                            dve.wait_ge(z2_psum, NG * n + q + 1)
                            dve.tensor_tensor(gate_e[:, cs], pZ[q][:, 0:w], be2_wide[:, 0:w],
                                              ALU.add).then_inc(u_made, 1)

                    def gates(n):
                        for q in range(NG):
                            cs, w = cols_of(q)
                            dve.wait_ge(log2_made, NG * n + q + 1)
                            dve.scalar_tensor_tensor(gate_e[:, cs], gate_e[:, cs], 0.0, lg2[:, cs],
                                                     ALU.max, ALU.add)

                    def make_hot(h, n, window, used):
                        dve.wait_ge(hot_used[h], used)
                        a, b = HALVES[h]
                        d = dst_f[:, bass.ds(n, 1), a:b].rearrange("p o j -> p (o j)")
                        dve.scalar_tensor_tensor(
                            hots[h], d.unsqueeze(2).to_broadcast([P, b - a, WIN]),
                            win_base[:, bass.ds(window, 1)],
                            iota_row[:, :].unsqueeze(1).to_broadcast([P, b - a, WIN]),
                            ALU.subtract, ALU.is_equal).then_inc(hot_made[h], 1)

                    def add_up(n, g, u, values_ahead=True):
                        since, to, first = windows(dve, n, True)
                        if with_edges:
                            dve.wait_ge(gathered[u], 16 * took * (g + 1))
                            dve.sem_inc(waited, 1)
                            dve.drain()
                            h = big[:, u, :]
                            dve.scalar_tensor_tensor(h, gate_e[:, 0:SLOTS * F], -LOG2, h, ALU.add,
                                                     ALU.mult).then_inc(gated, 1)
                            if values_ahead:
                                dve.wait_ge(gated, n + 1)
                                second_values(n + 1)
                        dve.drain()
                        make_hot(0, n, first, since + 1)
                        with dve.Fori(since, to) as visit:
                            window = nc.s_assert_within(
                                visit - since + first, 0, NW - 1,
                                skip_runtime_bounds_check_because="a visit's window is that of a dst")
                            make_hot(1, n, window, visit + 1)
                            make_hot(0, n, window + 1, visit + 2)
                            dve.wait_ge(hot_used[1], visit + 2)
                            dve.wait_ge(acc_added, visit + 1)
                            a_w = acc[0:cols, bass.ds(window * WIN, WIN)]
                            dve.tensor_tensor(a_w, a_w, sums[0:cols, 0:WIN], ALU.add).then_inc(acc_added, 1)

                    def body(n, g, u, last=False):
                        if with_edges:
                            add_up(n, g, u)
                            gates(n + 1)
                            if not last:
                                first_activation(n + 2)
                        else:
                            pick(n + 1, 1 - u)
                            if not last:
                                digit_hots(n + 2, g + 1, u)
                            add_up(n, g, u)

                    if with_edges:
                        first_activation(0)
                        second_values(0)
                        gates(0)
                        first_activation(1)
                    else:
                        dve.memset(table0[:, V // P:, :], 0.0).then_inc(table_tail, 1)
                        for u in range(2):
                            dve.memset(msgs[u][:, SLOTS - SEL:, ONES:LO], 1.0)
                        dve.sem_inc(sel_taken, 2)
                        dve.sem_inc(sel_made, 2)
                        digit_hots(0, 0, 0)
                        pick(0, 0)
                        digit_hots(1, 0, 1)
                    with dve.Fori(0, NB // 2 - 1) as g:
                        for u in range(2):
                            body(2 * g + u, g, u)
                    body(NB - 3, NB // 2 - 1, 0)
                    body(NB - 2, NB // 2 - 1, 1, last=True)
                    add_up(NB - 1, NB // 2, 0, values_ahead=False)

        def wide(per_row):
            return per_row.unsqueeze(2).to_broadcast([SUB, NSUB, F])

        def norm_center(dve, y, var, var_made):
            dve.drain()
            dve.tensor_reduce(st_sum[:, :], y, AX.X, ALU.add)
            dve.drain()
            dve.tensor_scalar(st_mean[:, :], st_sum[:, :], 1.0 / F, None, ALU.mult)
            dve.drain()
            dve.tensor_tensor(y, y, wide(st_mean[:, :]), ALU.subtract)
            dve.drain()
            dve.tensor_tensor(sq[:, :, :], y, y, ALU.mult)
            dve.drain()
            dve.tensor_reduce(st_sum[:, :], sq[:, :, :], AX.X, ALU.add)
            dve.drain()
            dve.tensor_scalar(var, st_sum[:, :], 1.0 / F, EPS, ALU.mult, ALU.add).then_inc(var_made, 1)

        def inverse_root(act, o, var, made):
            act.activation(o, var, ACT.Ln)
            act.drain()
            act.activation(o, o, ACT.Exp, scale=-0.5).then_inc(made, 1)

        edge_phase("e1", p1_table, msgs, hot0, ROW0, ROW0, False)

        b_pre = sem("b_pre")
        b_sum_psum = sem("b_sum_psum")
        b_h = sem("b_h")
        b_h_psum = sem("b_h_psum")
        b_out = sem("b_out")
        b_store = [sem(f"b_store{b}") for b in range(2)]
        b_deg_out = sem("b_deg_out")
        b_deg_in = sem("b_deg_in")
        b_inv = sem("b_inv")
        b_inv_out = sem("b_inv_out")
        b_inv_in = sem("b_inv_in")
        with nc.Block() as block:
            @block.vector
            def _(dve):
                dve.wait_ge(b_deg_in, 16)
                dve.tensor_scalar(deg_wide[:, :], deg_wide[:, :], 1.0, None, ALU.max)
                dve.drain()
                dve.reciprocal(deg_wide[:, :], deg_wide[:, :]).then_inc(b_inv, 1)
                dve.wait_ge(b_inv_in, 16)

                def mean_and_root(c, g, b):
                    cs = bass.ds(c * CH, CH)
                    wait_freed(dve, b_h, c)
                    dve.sem_inc(waited, 1)
                    dve.drain()
                    dve.tensor_copy(inv_deg[:, :], inv_rows[:, cs])
                    dve.drain()
                    wait_chunk(dve, b_sum_psum, c)
                    dve.tensor_tensor(nT2[b][0:H, :], bank[2 + b][0:H, 0:CH], inv_deg[:, :], ALU.mult)
                    dve.drain()
                    dve.tensor_tensor(nT2[b][0:H, :], nT2[b][0:H, :], hT[:, cs], ALU.add).then_inc(b_pre, 1)

                def out_h1(c, g, b):
                    wait_chunk(dve, b_h_psum, c)
                    wait_stored(dve, b_store, c, g, b)
                    dve.sem_inc(waited, 1)
                    dve.tensor_copy(hT[:, bass.ds(c * CH, CH)], nT[b][0:H, :])
                    table_rows(dve, o_small[b], bank[b], b_out)

                chunks_of(dve, (mean_and_root, 0), (out_h1, 2))

            @block.scalar
            def _(act):
                def h1(c, g, b):
                    wait_chunk(act, b_pre, c)
                    wait_freed(act, b_out, c)
                    act.activation(nT[b][0:H, :], nT2[b][0:H, :], ACT.Tanh).then_inc(b_h, 1)
                chunks_of(act, (h1, 0))

            @block.tensor
            def _(pe):
                def turn_h1(c, g, b):
                    wait_chunk(pe, b_h, c)
                    wait_freed(pe, b_out, c)
                    pe.sem_inc(waited, 1)
                    for s in range(NSUB):
                        last = pe.transpose(bank[b][0:SUB, s * H:(s + 1) * H], nT[b][0:H, s * SUB:(s + 1) * SUB],
                                            ident[0:H, 0:H])
                    last.then_inc(b_h_psum, 1)

                def add_rows(c, g, b):
                    wait_freed(pe, b_pre, c)
                    pe.matmul(bank[2 + b][:, 0:CH], add_parts[:, :], acc[:, bass.ds(c * CH, CH)], start=True,
                              stop=True).then_inc(b_sum_psum, 1)
                chunks_of(pe, (add_rows, 0), (turn_h1, 1))

            @block.sync
            def _(sp):
                sp.dma_start(deg_dram[0:1, :], acc[ONES:ONES + 1, :]).then_inc(b_deg_out, 16)
                sp.wait_ge(b_deg_out, 16)
                sp.dma_start(deg_wide[:, :], deg_dram[0, :].rearrange("(p w) -> p w", p=P)).then_inc(b_deg_in, 16)
                sp.wait_ge(b_inv, 1)
                sp.dma_start(deg_dram[1, :].rearrange("(p w) -> p w", p=P), deg_wide[:, :]).then_inc(b_inv_out, 16)
                sp.wait_ge(b_inv_out, 16)
                sp.dma_start(inv_rows, deg_dram[1:2, 0:V].to_broadcast([H, V])).then_inc(b_inv_in, 16)

                def store_h1(c, g, b):
                    wait_chunk(sp, b_out, c)
                    sp.dma_start(h1_v[c], o_small[b][:, :, :]).then_inc(b_store[b], 16)
                chunks_of(sp, (store_h1, 0))
                all_stored(sp, b_store)

            @block.gpsimd
            def _(pool):
                pool.wait_ge(b_deg_out, 16)
                with pool.Fori(0, NC) as c:
                    wait_chunk(pool, b_pre, c)
                    pool.sem_inc(waited, 1)
                    pool.tensor_copy(acc[:, bass.ds(c * CH, CH)], zeros[:, :])

        edge_phase("e2", h1_table, msgs, hot0, ROW0, ROW0, False)

        c_mean = sem("c_mean")
        c_sum_psum = sem("c_sum_psum")
        c_root = sem("c_root")
        c_o_psum = sem("c_o_psum")
        c_tanh = sem("c_tanh")
        c_var = sem("c_var")
        with nc.Block() as block:
            @block.vector
            def _(dve):
                def mean(c, g, b):
                    cs = bass.ds(c * CH, CH)
                    wait_freed(dve, c_o_psum, c)
                    dve.sem_inc(waited, 1)
                    dve.drain()
                    dve.tensor_copy(inv_deg[:, :], inv_rows[:, cs])
                    dve.drain()
                    wait_chunk(dve, c_sum_psum, c)
                    dve.tensor_tensor(nT2[b][0:H, :], bank[2 + b][0:H, 0:CH], inv_deg[:, :],
                                      ALU.mult).then_inc(c_mean, 1)

                def residual(c, g, b):
                    wait_chunk(dve, c_tanh, c)
                    y = x1[:, bass.ds(c * NSUB, NSUB), :]
                    dve.tensor_tensor(y, yv[b][:, :, :], y, ALU.add)
                    norm_center(dve, y, x1_var[:, bass.ds(c * NSUB, NSUB)], c_var)

                chunks_of(dve, (mean, 0), (residual, 1))

            @block.gpsimd
            def _(pool):
                def copies(c, g, b):
                    wait_freed(pool, c_o_psum, c)
                    pool.sem_inc(waited, 1)
                    pool.tensor_copy(h_chunk[b][:, :], hT[:, bass.ds(c * CH, CH)]).then_inc(c_root, 1)
                    wait_chunk(pool, c_mean, c)
                    pool.sem_inc(waited, 1)
                    pool.tensor_copy(acc[:, bass.ds(c * CH, CH)], zeros[:, :])
                chunks_of(pool, (copies, 0))

            @block.scalar
            def _(act):
                def o_tanh(c, g, b):
                    wait_chunk(act, c_o_psum, c)
                    wait_freed(act, c_var, c)
                    act.activation(yv[b][:, :, :], features(bank[b]), ACT.Tanh).then_inc(c_tanh, 1)
                chunks_of(act, (o_tanh, 0))

            @block.tensor
            def _(pe):
                def products(c, g, b):
                    wait_chunk(pe, c_mean, c)
                    wait_chunk(pe, c_root, c)
                    wait_freed(pe, c_tanh, c)
                    pe.sem_inc(waited, 1)
                    for s in range(NSUB):
                        o = bank[b][0:SUB, s * F:(s + 1) * F]
                        pe.matmul(o, nT2[b][0:H, s * SUB:(s + 1) * SUB], w2a[:, :], start=True, stop=False)
                        pe.matmul(o, h_chunk[b][:, s * SUB:(s + 1) * SUB], w2r[:, :], start=False, stop=False)
                        last = pe.matmul(o, ones_row[:, 0:SUB], r_b2[:, :], start=False, stop=True)
                    last.then_inc(c_o_psum, 1)

                def add_rows(c, g, b):
                    wait_freed(pe, c_mean, c)
                    pe.matmul(bank[2 + b][:, 0:CH], add_parts[:, :], acc[:, bass.ds(c * CH, CH)], start=True,
                              stop=True).then_inc(c_sum_psum, 1)
                chunks_of(pe, (add_rows, 0), (products, 1))

        f_rstd = sem("f_rstd")
        f_x1 = sem("f_x1")
        f_xT_psum = sem("f_xT_psum")
        f_xT = sem("f_xT")
        f_hn_psum = sem("f_hn_psum")
        f_out = sem("f_out")
        f_store = [sem(f"f_store{b}") for b in range(2)]
        with nc.Block() as block:
            @block.scalar
            def _(act):
                inverse_root(act, x1_rstd[:, :], x1_var[:, :], f_rstd)

                def x1_turned(c, g, b):
                    wait_chunk(act, f_xT_psum, c)
                    act.copy(nT[b][:, :], bank[b][0:F, 0:CH]).then_inc(f_xT, 1)

                def out_hn(c, g, b):
                    wait_chunk(act, f_hn_psum, c)
                    wait_stored(act, f_store, c, g, b)
                    act.copy(o_wide[b][:, :, :], features(bank[2 + b])).then_inc(f_out, 1)

                chunks_of(act, (x1_turned, 0), (out_hn, 1))

            @block.vector
            def _(dve):
                dve.wait_ge(f_rstd, 1)

                def divide(c, g, b):
                    y = x1[:, bass.ds(c * NSUB, NSUB), :]
                    dve.tensor_tensor(y, y, wide(x1_rstd[:, bass.ds(c * NSUB, NSUB)]), ALU.mult)
                    wait_freed(dve, f_xT_psum, c)
                    if later(c):
                        dve.sem_inc(waited, 1)
                    dve.drain()
                    dve.tensor_copy(yv[b][:, :, :], y).then_inc(f_x1, 1)
                chunks_of(dve, (divide, 0))

            @block.tensor
            def _(pe):
                def turn_x1(c, g, b):
                    wait_chunk(pe, f_x1, c)
                    wait_freed(pe, f_xT, c)
                    pe.sem_inc(waited, 1)
                    for s in range(NSUB):
                        last = pe.transpose(bank[b][0:F, s * SUB:(s + 1) * SUB], yv[b][:, s, :],
                                            ident[0:SUB, 0:SUB])
                    last.then_inc(f_xT_psum, 1)

                def products(c, g, b):
                    wait_chunk(pe, f_xT, c)
                    wait_freed(pe, f_out, c)
                    pe.sem_inc(waited, 1)
                    for s in range(NSUB):
                        o = bank[2 + b][0:SUB, s * F:(s + 1) * F]
                        pe.matmul(o, nT[b][:, s * SUB:(s + 1) * SUB], wn[:, :], start=True, stop=False)
                        last = pe.matmul(o, ones_row[:, 0:SUB], r_bn[:, :], start=False, stop=True)
                    last.then_inc(f_hn_psum, 1)

                chunks_of(pe, (turn_x1, 0), (products, 1))

            @block.sync
            def _(sp):
                def store_hn(c, g, b):
                    wait_chunk(sp, f_out, c)
                    sp.dma_start(hn_v[c], o_wide[b][:, :, :]).then_inc(f_store[b], 16)
                chunks_of(sp, (store_hn, 0))
                all_stored(sp, f_store)

            @block.gpsimd
            def _(pool):
                for u in range(2):
                    pool.memset(x_e[u][:, SLOTS * F:], 0.0)

        edge_phase("e3", hn_table, rows, [h[:, :, :] for h in hot], F, F, True)

        d_c_psum = sem("d_c_psum")
        d_log = sem("d_log")
        d_s = sem("d_s")
        d_o_psum = sem("d_o_psum")
        d_y = sem("d_y")
        d_var = sem("d_var")
        d_rstd = sem("d_rstd")
        d_out = sem("d_out")
        d_store = [sem(f"d_store{b}") for b in range(2)]
        with nc.Block() as block:
            @block.tensor
            def _(pe):
                def first(c, g, b):
                    wait_freed(pe, d_s, c)
                    pe.matmul(bank[b][:, 0:CH], wc[:, :], acc[:, bass.ds(c * CH, CH)], start=True,
                              stop=True).then_inc(d_c_psum, 1)

                def second(c, g, b):
                    wait_chunk(pe, d_s, c)
                    wait_freed(pe, d_y, c)
                    pe.sem_inc(waited, 1)
                    for s in range(NSUB):
                        o = bank[2 + b][0:SUB, s * F:(s + 1) * F]
                        pe.matmul(o, nT[b][:, s * SUB:(s + 1) * SUB], wp[:, :], start=True, stop=False)
                        last = pe.matmul(o, ones_row[:, 0:SUB], r_bp[:, :], start=False, stop=True)
                    last.then_inc(d_o_psum, 1)

                chunks_of(pe, (first, 0), (second, 1))

            @block.scalar
            def _(act):
                act.preload_act_table_set("natural_log_exp_and_others")

                def log(c, g, b):
                    wait_chunk(act, d_c_psum, c)
                    wait_freed(act, d_s, c)
                    act.activation(nT2[b][:, :], bank[b][0:F, 0:CH], ACT.Abs, bias=c_bc[:, :])
                    act.drain()
                    act.activation(nT2[b][:, :], nT2[b][:, :], ACT.Exp, scale=-1.0)
                    act.drain()
                    act.activation(nT2[b][:, :], nT2[b][:, :], ACT.Ln, bias=1.0).then_inc(d_log, 1)

                def root(c, g, b):
                    wait_chunk(act, d_var, c)
                    wait_freed(act, d_out, c)
                    inverse_root(act, st_rstd[b][:, :], st_var[b][:, :], d_rstd)

                chunks_of(act, (log, 0), (root, 2))

            @block.vector
            def _(dve):
                def softplus(c, g, b):
                    wait_chunk(dve, d_log, c)
                    wait_freed(dve, d_o_psum, c)
                    dve.scalar_tensor_tensor(nT[b][:, :], bank[b][0:F, 0:CH], n_bc[:, :], nT2[b][:, :], ALU.max,
                                             ALU.add)
                    dve.drain()
                    dve.tensor_scalar(nT[b][:, :], nT[b][:, :], bc_off[:, :], None, ALU.add).then_inc(d_s, 1)

                def residual(c, g, b):
                    wait_chunk(dve, d_o_psum, c)
                    dve.tensor_tensor(yv[b][:, :, :], features(bank[2 + b]), x1[:, bass.ds(c * NSUB, NSUB), :],
                                      ALU.add).then_inc(d_y, 1)
                    norm_center(dve, yv[b][:, :, :], st_var[b][:, :], d_var)

                def divide(c, g, b):
                    wait_chunk(dve, d_rstd, c)
                    wait_stored(dve, d_store, c, g, b)
                    dve.tensor_tensor(o_wide[b][:, :, :], yv[b][:, :, :], wide(st_rstd[b][:, :]),
                                      ALU.mult).then_inc(d_out, 1)

                chunks_of(dve, (softplus, 0), (divide, 2), (residual, 1))

            @block.sync
            def _(sp):
                def store_out(c, g, b):
                    wait_chunk(sp, d_out, c)
                    sp.dma_start(out_v[c], o_wide[b][:, :, :]).then_inc(d_store[b], 16)
                chunks_of(sp, (store_out, 0))
                all_stored(sp, d_store)


_INS = ["x", "src", "dst", "edge", "W_lin", "b_lin", "W1_agg", "W1_root", "b1", "W2_agg", "W2_root", "b2",
        "WnT", "bn", "We1T", "be1", "We2T", "be2", "WcT", "bc", "WpT", "bp"]


def kernel(x, src, dst, edge_attr_64, L0_gnn_W_lin, L0_gnn_b_lin, L0_gnn_W1_agg, L0_gnn_W1_root, L0_gnn_b1,
           L0_gnn_W2_agg, L0_gnn_W2_root, L0_gnn_b2, L1_gnn_Wn, L1_gnn_bn, L1_gnn_We1, L1_gnn_be1, L1_gnn_We2,
           L1_gnn_be2, L1_gnn_Wc, L1_gnn_bc, L1_gnn_Wp, L1_gnn_bp):
    import numpy as np
    import concourse.bacc as bacc
    from concourse.bass_utils import run_bass_kernel_spmd

    def col(a):
        return np.asarray(a).reshape(-1, 1)

    def row(a):
        return np.asarray(a).reshape(1, -1)

    def turned(a):
        return np.asarray(a).T

    values = [x, src, dst, edge_attr_64, L0_gnn_W_lin, col(L0_gnn_b_lin), L0_gnn_W1_agg, L0_gnn_W1_root,
              col(L0_gnn_b1), L0_gnn_W2_agg, L0_gnn_W2_root, row(L0_gnn_b2), turned(L1_gnn_Wn), row(L1_gnn_bn),
              turned(L1_gnn_We1), col(L1_gnn_be1), turned(L1_gnn_We2), row(L1_gnn_be2), turned(L1_gnn_Wc),
              col(L1_gnn_bc), turned(L1_gnn_Wp), row(L1_gnn_bp)]
    nc = bacc.Bacc("TRN2", target_bir_lowering=False, num_devices=1)
    arrays, args = {}, []
    for name, value in zip(_INS, values):
        a = np.ascontiguousarray(value)
        arrays[f"in_{name}"] = a
        args.append(nc.dram_tensor(f"in_{name}", a.shape, mybir.dt.from_np(a.dtype), kind="ExternalInput").ap())
    args.append(nc.dram_tensor("out_dram", (V, F), F32, kind="ExternalOutput").ap())
    gnn_kernel(nc, *args)
    result = run_bass_kernel_spmd(nc, [arrays], core_ids=[0])
    return result.results[0]["out_dram"]
```
